# Optimizing a Trainium2 kernel written in Bass

```python
import numpy as np
import jax
import jax.numpy as jnp

def _softmax(x, axis=-1):
    return jax.nn.softmax(x, axis=axis)

def _gelu(x):
    return jax.nn.gelu(x, approximate=True)

def _silu(x):
    return jax.nn.silu(x)

def _sigmoid(x):
    return jax.nn.sigmoid(x)

def _layernorm(x, axis=-1, eps=1e-05):
    m = jnp.mean(x, axis=axis, keepdims=True)
    v = jnp.var(x, axis=axis, keepdims=True)
    return (x - m) / jnp.sqrt(v + eps)

def _scatter_add(tgt, idx, src, axis=0):
    return tgt.at[idx].add(src)

def _segment_sum(src, seg, n):
    return jax.ops.segment_sum(src, seg, n)
kernel_name = 'mk_seq_preln_d2_jaxref_r8_130f69'

def setup_inputs(seed: int=0):
    np.random.seed(seed)
    _w = jnp.asarray

    def _L0_attn_setup():
        import jax, jax.numpy as jnp
        import numpy as np
        B, S, D = (4, 256, 256)
        H = 16
        HD = D // H
        key = jax.random.key(seed)
        ks = jax.random.split(key, 5)
        scale = 1.0 / np.sqrt(D)
        return {'x': jax.random.normal(ks[0], (B, S, D), dtype=jnp.float32), 'wq': jax.random.normal(ks[1], (D, D), dtype=jnp.float32) * scale, 'wk': jax.random.normal(ks[2], (D, D), dtype=jnp.float32) * scale, 'wv': jax.random.normal(ks[3], (D, D), dtype=jnp.float32) * scale, 'wo': jax.random.normal(ks[4], (D, D), dtype=jnp.float32) * scale}
    _L0_attn_in = _L0_attn_setup()

    def _L0_ffn_setup():
        import jax, jax.numpy as jnp
        import numpy as np
        D_MODEL = 256
        HIDDEN = int(2 * D_MODEL * 4 / 3)

        def ternary_quant(w):
            s = jnp.mean(jnp.abs(w))
            q = jnp.clip(jnp.round(w / s), -1.0, 1.0) * s
            return w + jax.lax.stop_gradient(q - w)
        key = jax.random.key(seed)
        k0, k1, k2, k3 = jax.random.split(key, 4)
        x = jax.random.normal(k0, (4, 512, D_MODEL), dtype=jnp.float32)
        std_in = 1.0 / np.sqrt(D_MODEL)
        std_h = 1.0 / np.sqrt(HIDDEN)
        w1 = jax.random.uniform(k1, (HIDDEN, D_MODEL), jnp.float32, -std_in, std_in)
        w3 = jax.random.uniform(k2, (HIDDEN, D_MODEL), jnp.float32, -std_in, std_in)
        w2 = jax.random.uniform(k3, (D_MODEL, HIDDEN), jnp.float32, -std_h, std_h)
        return {'x': x, 'w1': w1, 'w3': w3, 'w2': w2}
    _L0_ffn_in = _L0_ffn_setup()

    def _L1_attn_setup():
        import jax, jax.numpy as jnp
        import numpy as np
        import math
        N_HEADS = 32
        N_GROUPS = 8
        D_HEAD = 64
        D_MODEL = 256

        def _rope(x):
            S, D = (x.shape[-2], x.shape[-1])
            inv_freq = 1.0 / 10000.0 ** (jnp.arange(0, D, 2, dtype=jnp.float32) / D)
            freqs = jnp.arange(S, dtype=jnp.float32)[:, None] * inv_freq[None, :]
            cos = jnp.repeat(jnp.cos(freqs), 2, axis=-1)
            sin = jnp.repeat(jnp.sin(freqs), 2, axis=-1)
            x2 = x.reshape(*x.shape[:-1], D // 2, 2)
            rot = jnp.stack([-x2[..., 1], x2[..., 0]], axis=-1).reshape(x.shape)
            return x * cos + rot * sin
        key = jax.random.key(seed)
        ks = jax.random.split(key, 6)
        hidden_states = jax.random.normal(ks[0], (2, 256, D_MODEL), dtype=jnp.float32)
        s = 0.02
        Wq = jax.random.normal(ks[1], (D_MODEL, N_HEADS * D_HEAD), dtype=jnp.float32) * s
        Wk = jax.random.normal(ks[2], (D_MODEL, N_GROUPS * D_HEAD), dtype=jnp.float32) * s
        Wv = jax.random.normal(ks[3], (D_MODEL, N_GROUPS * D_HEAD), dtype=jnp.float32) * s
        Wo = jax.random.normal(ks[4], (N_HEADS * D_HEAD, D_MODEL), dtype=jnp.float32) * s
        bo = jnp.zeros((D_MODEL,), dtype=jnp.float32)
        return {'hidden_states': hidden_states, 'Wq': Wq, 'Wk': Wk, 'Wv': Wv, 'Wo': Wo, 'bo': bo}
    _L1_attn_in = _L1_attn_setup()

    def _L1_ffn_setup():
        import jax, jax.numpy as jnp
        import numpy as np
        B, S, D, K, R = (4, 256, 256, 8, 64)
        key = jax.random.key(seed)
        ks = jax.random.split(key, 7)
        x = jax.random.normal(ks[0], (B, S, D), dtype=jnp.float32)
        U = jax.random.normal(ks[1], (K, D, R), dtype=jnp.float32) * 0.02
        V = jax.random.normal(ks[2], (K, R, D), dtype=jnp.float32) * 0.02
        W1 = jax.random.normal(ks[3], (D, D), dtype=jnp.float32) * 0.02
        b1 = jnp.zeros((D,), dtype=jnp.float32)
        W2 = jax.random.normal(ks[4], (D, K), dtype=jnp.float32) * 0.02
        b2 = jnp.zeros((K,), dtype=jnp.float32)
        return {'x': x, 'U': U, 'V': V, 'W1': W1, 'b1': b1, 'W2': W2, 'b2': b2}
    _L1_ffn_in = _L1_ffn_setup()
    _d = {'L0_attn_x': _L0_attn_in['x'], 'L0_attn_wq': _L0_attn_in['wq'], 'L0_attn_wk': _L0_attn_in['wk'], 'L0_attn_wv': _L0_attn_in['wv'], 'L0_attn_wo': _L0_attn_in['wo'], 'L0_ffn_w1': _L0_ffn_in['w1'], 'L0_ffn_w3': _L0_ffn_in['w3'], 'L0_ffn_w2': _L0_ffn_in['w2'], 'L1_attn_Wq': _L1_attn_in['Wq'], 'L1_attn_Wk': _L1_attn_in['Wk'], 'L1_attn_Wv': _L1_attn_in['Wv'], 'L1_attn_Wo': _L1_attn_in['Wo'], 'L1_attn_bo': _L1_attn_in['bo'], 'L1_ffn_U': _L1_ffn_in['U'], 'L1_ffn_V': _L1_ffn_in['V'], 'L1_ffn_W1': _L1_ffn_in['W1'], 'L1_ffn_b1': _L1_ffn_in['b1'], 'L1_ffn_W2': _L1_ffn_in['W2'], 'L1_ffn_b2': _L1_ffn_in['b2']}
    _x0 = _d['L0_attn_x']
    _d['L0_attn_x'] = jax.random.normal(jax.random.fold_in(jax.random.key(seed), 1), (2, 1024, 256), dtype=_x0.dtype)
    del _x0
    return _d

def reference(L0_attn_x, L0_attn_wq, L0_attn_wk, L0_attn_wv, L0_attn_wo, L0_ffn_w1, L0_ffn_w3, L0_ffn_w2, L1_attn_Wq, L1_attn_Wk, L1_attn_Wv, L1_attn_Wo, L1_attn_bo, L1_ffn_U, L1_ffn_V, L1_ffn_W1, L1_ffn_b1, L1_ffn_W2, L1_ffn_b2):

    def _L0_attn_ref(x, wq, wk, wv, wo):
        import jax, jax.numpy as jnp
        import numpy as np
        B, S, D = (4, 256, 256)
        H = 16
        HD = D // H
        b, s, d = x.shape
        q = (x @ wq.T).reshape(b, s, H, HD).transpose(0, 2, 1, 3)
        k = (x @ wk.T).reshape(b, s, H, HD).transpose(0, 2, 1, 3)
        v = (x @ wv.T).reshape(b, s, H, HD).transpose(0, 2, 1, 3)
        scores = jnp.einsum('bhqd,bhkd->bhqk', q, k) / np.sqrt(HD)
        causal = jnp.tril(jnp.ones((s, s), dtype=bool))
        scores = jnp.where(causal, scores, -jnp.inf)
        prob = jax.nn.softmax(scores, axis=-1)
        out = jnp.einsum('bhqk,bhkd->bhqd', prob, v)
        out = out.transpose(0, 2, 1, 3).reshape(b, s, d)
        return out @ wo.T

    def _L0_ffn_ref(x, w1, w3, w2):
        import jax, jax.numpy as jnp
        import numpy as np
        D_MODEL = 256
        HIDDEN = int(2 * D_MODEL * 4 / 3)

        def ternary_quant(w):
            s = jnp.mean(jnp.abs(w))
            q = jnp.clip(jnp.round(w / s), -1.0, 1.0) * s
            return w + jax.lax.stop_gradient(q - w)
        w1q = ternary_quant(w1)
        w3q = ternary_quant(w3)
        w2q = ternary_quant(w2)
        h1 = jnp.einsum('bsd,hd->bsh', x, w1q)
        h3 = jnp.einsum('bsd,hd->bsh', x, w3q)
        g = jax.nn.silu(h1) * h3
        return jnp.einsum('bsh,dh->bsd', g, w2q)

    def _L1_attn_ref(hidden_states, Wq, Wk, Wv, Wo, bo):
        import jax, jax.numpy as jnp
        import numpy as np
        import math
        N_HEADS = 32
        N_GROUPS = 8
        D_HEAD = 64
        D_MODEL = 256

        def _rope(x):
            S, D = (x.shape[-2], x.shape[-1])
            inv_freq = 1.0 / 10000.0 ** (jnp.arange(0, D, 2, dtype=jnp.float32) / D)
            freqs = jnp.arange(S, dtype=jnp.float32)[:, None] * inv_freq[None, :]
            cos = jnp.repeat(jnp.cos(freqs), 2, axis=-1)
            sin = jnp.repeat(jnp.sin(freqs), 2, axis=-1)
            x2 = x.reshape(*x.shape[:-1], D // 2, 2)
            rot = jnp.stack([-x2[..., 1], x2[..., 0]], axis=-1).reshape(x.shape)
            return x * cos + rot * sin
        N, S, _ = hidden_states.shape
        n_rep = N_HEADS // N_GROUPS
        q = (hidden_states @ Wq).reshape(N, S, N_HEADS, D_HEAD).transpose(0, 2, 1, 3)
        k = (hidden_states @ Wk).reshape(N, S, N_GROUPS, D_HEAD).transpose(0, 2, 1, 3)
        v = (hidden_states @ Wv).reshape(N, S, N_GROUPS, D_HEAD).transpose(0, 2, 1, 3)
        q = _rope(q)
        k = _rope(k)
        k = jnp.repeat(k, n_rep, axis=1)
        v = jnp.repeat(v, n_rep, axis=1)
        scores = jnp.einsum('bhsd,bhtd->bhst', q, k)
        slopes = 2.0 ** (-(jnp.arange(1, N_HEADS + 1, dtype=jnp.float32) * 8.0 / N_HEADS))
        pos = jnp.arange(S, dtype=jnp.float32)
        alibi = -jnp.abs(pos[:, None] - pos[None, :])[None] * slopes[:, None, None]
        scores = (scores + alibi[None]) / math.sqrt(D_HEAD)
        scores = 30.0 * jnp.tanh(scores / 30.0)
        causal = jnp.tril(jnp.ones((S, S), dtype=bool))
        scores = jnp.where(causal[None, None], scores, -jnp.inf)
        probs = jax.nn.softmax(scores, axis=-1)
        ctx = jnp.einsum('bhst,bhtd->bhsd', probs, v)
        ctx = ctx.transpose(0, 2, 1, 3).reshape(N, S, N_HEADS * D_HEAD)
        return ctx @ Wo + bo

    def _L1_ffn_ref(x, U, V, W1, b1, W2, b2):
        import jax, jax.numpy as jnp
        import numpy as np
        B, S, D, K, R = (4, 256, 256, 8, 64)
        h = jax.nn.relu(jnp.einsum('bsd,de->bse', x, W1) + b1)
        alpha = jax.nn.softmax(jnp.einsum('bse,ek->bsk', h, W2) + b2, axis=-1)
        vx = jnp.einsum('krd,bsd->bskr', V, x)
        uvx = jnp.einsum('kdr,bskr->bskd', U, vx)
        out = jnp.einsum('bsk,bskd->bsd', alpha, uvx)
        return out
    x = L0_attn_x
    x = x + _L0_attn_ref(_layernorm(x, axis=-1), L0_attn_wq, L0_attn_wk, L0_attn_wv, L0_attn_wo)
    x = x + _L0_ffn_ref(_layernorm(x, axis=-1), L0_ffn_w1, L0_ffn_w3, L0_ffn_w2)
    x = x + _L1_attn_ref(_layernorm(x, axis=-1), L1_attn_Wq, L1_attn_Wk, L1_attn_Wv, L1_attn_Wo, L1_attn_bo)
    x = x + _L1_ffn_ref(_layernorm(x, axis=-1), L1_ffn_U, L1_ffn_V, L1_ffn_W1, L1_ffn_b1, L1_ffn_W2, L1_ffn_b2)
    return x

_drawn_inputs = setup_inputs


def setup_inputs(seed=0):
    import zlib

    import numpy as np

    out = dict(_drawn_inputs(seed))
    spreads = {'L1_attn_bo': (0.0, 0.1), 'L1_ffn_b1': (0.0, 0.8), 'L1_ffn_b2': (0.0, 0.8)}
    factors = {'L1_attn_Wq': 8.0,
     'L1_attn_Wk': 8.0,
     'L1_ffn_U': 3.177,
     'L1_ffn_V': 3.175,
     'L1_ffn_W1': 8.0,
     'L1_ffn_W2': 8.0}
    for name, (base, spread) in spreads.items():
        noise = np.random.default_rng([zlib.crc32(name.encode()), seed]).standard_normal(out[name].shape)
        drawn = base * np.exp(spread * noise) if base else spread * noise
        out[name] = jnp.asarray(drawn.astype(out[name].dtype))
    for name, factor in factors.items():
        out[name] = (out[name] * factor).astype(out[name].dtype)
    return out
```

```python
import concourse.bass as bass
from concourse import mybir
from contextlib import ExitStack

FP32 = mybir.dt.float32
FP32R = mybir.dt.float32r
BF16 = mybir.dt.bfloat16
ALU = mybir.AluOpType
ACT = mybir.ActivationFunctionType
AXIS = mybir.AxisListType

P = 128
BATCH, SEQ, DM = 2, 1024, 256
TOK = BATCH * SEQ
TT = TOK // P
KC = DM // P
NB = SEQ // P
H0, HD0 = 16, 16
H1, G1, HD1 = 32, 8, 64
REP = H1 // G1
HID = int(2 * DM * 4 / 3)
HC = -(-HID // P)
HLAST = HID - (HC - 1) * P
EXPERTS, RANK = 8, 64
ER = EXPERTS * RANK // P
AUX = 6
EPS = 1e-5
LOWEST = -3e38


class Chain:

    def __init__(self, engine, semaphore, base=0):
        self.engine, self.semaphore, self.n, self.base = engine, semaphore, 0, base

    def link(self, instruction):
        self.n += 1
        instruction.then_inc(self.semaphore, 1)
        self.engine.wait_ge(self.semaphore, self.base + self.n)


def layer_norm(nc, name, x, xh, xl, ident, psum):
    with ExitStack() as ctx:
        sb = lambda n, s, d=FP32: ctx.enter_context(nc.sbuf_tensor(f"{name}_{n}", s, d))
        sem = lambda n: ctx.enter_context(nc.semaphore(f"{name}_{n}"))
        stats = sb("stats", [P, TT, 6])
        mean_var = sb("mean_var", [P, TT, 2])
        var_eps = sb("var_eps", [P, TT])
        std = sb("std", [P, TT])
        rstd = sb("rstd", [P, TT])
        xn = sb("xn", [P, 8, DM])
        v_seq, std_ready, rows_ready, turned, high_ready, low_ready = map(
            sem, ("v_seq", "std_ready", "rows_ready", "turned", "high_ready", "low_ready"))
        with nc.Block() as block:
            @block.vector
            def _(dve):
                for t in range(TT):
                    last = nc.vector.bn_stats(stats[:, t, :], x[:, t, :])
                last.then_inc(v_seq, 1)
                dve.wait_ge(v_seq, 1)
                for t in range(TT):
                    last = nc.vector.bn_aggr(mean_var[:, t, :], stats[:, t, :])
                last.then_inc(v_seq, 1)
                dve.wait_ge(v_seq, 2)
                nc.vector.tensor_scalar(var_eps[:, :], mean_var[:, :, 1], EPS, None, ALU.add).then_inc(v_seq, 1)
                dve.wait_ge(std_ready, 1)
                nc.vector.reciprocal(rstd[:, :], std[:, :]).then_inc(v_seq, 1)
                dve.wait_ge(v_seq, 4)
                for half in range(2):
                    for q in range(2):
                        for t in range(4):
                            tile = 8 * half + 4 * q + t
                            if half == 1 and t == 0:
                                dve.wait_ge(turned, q + 1)
                            last = nc.vector.tensor_scalar(xn[:, 4 * q + t, :], x[:, tile, :], mean_var[:, tile, 0:1],
                                                           rstd[:, tile:tile + 1], ALU.subtract, ALU.mult)
                        last.then_inc(rows_ready, 1)
                    for q in range(2):
                        group = 2 * half + q
                        dve.wait_ge(high_ready, group + 1)
                        for c in range(KC):
                            cols = slice(group * 512, group * 512 + 512)
                            last = nc.vector.tensor_tensor(xl[:, c, cols], psum[:, 2 * q + c, :], xh[:, c, cols],
                                                           ALU.subtract)
                        last.then_inc(low_ready, 1)

            @block.scalar
            def _(act):
                act.wait_ge(v_seq, 3)
                nc.scalar.activation(std[:, :], var_eps[:, :], ACT.Sqrt).then_inc(std_ready, 1)
                for group in range(4):
                    act.wait_ge(turned, group + 1)
                    for c in range(KC):
                        cols = slice(group * 512, group * 512 + 512)
                        last = nc.scalar.activation(xh[:, c, cols], psum[:, 2 * (group % 2) + c, :], ACT.Copy)
                    last.then_inc(high_ready, 1)

            @block.tensor
            def _(pe):
                for group in range(4):
                    pe.wait_ge(rows_ready, group + 1)
                    if group >= 2:
                        pe.wait_ge(low_ready, group - 1)
                    for t in range(4):
                        for c in range(KC):
                            last = nc.tensor.transpose(psum[:, 2 * (group % 2) + c, t * P:(t + 1) * P],
                                                       xn[:, 4 * (group % 2) + t, c * P:(c + 1) * P], ident[:, :])
                    last.then_inc(turned, 1)


def three_pass(nc, out, pairs):
    terms = []
    for (ah, al), (bh, bl) in pairs:
        terms += [(ah, bh), (al, bh), (ah, bl)]
    for n, (a, b) in enumerate(terms):
        last = nc.tensor.matmul(out, a, b, start=(n == 0), stop=(n == len(terms) - 1))
    return last


def layer0_attention(nc, x, ident, ident_b, mask_q, mask_k, psum, wq0, wk0, wv0, wo0):
    with ExitStack() as outer:
        osb = lambda n, s, d=FP32: outer.enter_context(nc.sbuf_tensor(f"a0_{n}", s, d))
        qh, ql = osb("qh", [P, 4, SEQ]), osb("ql", [P, 4, SEQ])
        kh, kl = osb("kh", [P, 4, SEQ]), osb("kl", [P, 4, SEQ])
        v0 = osb("v0", [P, TT, DM])

        with ExitStack() as ctx:
            sb = lambda n, s, d=FP32: ctx.enter_context(nc.sbuf_tensor(f"p0_{n}", s, d))
            sem = lambda n: ctx.enter_context(nc.semaphore(f"p0_{n}"))
            xh, xl = sb("xh", [P, KC, TOK], FP32R), sb("xl", [P, KC, TOK], FP32R)
            layer_norm(nc, "n0", x, xh, xl, ident, psum)
            raw = [sb(f"raw{n}", [P, KC, DM]) for n in range(3)]
            wh = [sb(f"wh{n}", [P, KC, DM], FP32R) for n in range(3)]
            wl = [sb(f"wl{n}", [P, KC, DM], FP32R) for n in range(3)]
            loaded = [sem(f"loaded{n}") for n in range(3)]
            split, product, high_ready, bank_free, v_seq = map(
                sem, ("split", "product", "high_ready", "bank_free", "v_seq"))
            dst = {0: (qh, ql), 1: (kh, kl)}
            items = [(w, c, tb) for w in range(2) for c in range(KC) for tb in range(4)]
            items += [(2, None, t) for t in range(TT)]
            BANKS = 8

            with nc.Block() as block:
                @block.sync
                def _(sp):
                    for n, w in enumerate((wq0, wk0, wv0)):
                        sp.dma_start(raw[n][:, :, :], w).then_inc(loaded[n], 16)

                @block.tensor
                def _(pe):
                    for n, (w, c, t) in enumerate(items):
                        if n == 0 or items[n - 1][0] != w:
                            pe.wait_ge(split, w + 1)
                        if n >= BANKS:
                            pe.wait_ge(bank_free, n - BANKS + 1)
                        if w < 2:
                            m = slice(c * P, (c + 1) * P)
                            cols = slice(t * 512, t * 512 + 512)
                            three_pass(nc, psum[:, n % BANKS, :],
                                       [((wh[w][:, k, m], wl[w][:, k, m]), (xh[:, k, cols], xl[:, k, cols]))
                                        for k in range(KC)]).then_inc(product, 1)
                        else:
                            cols = slice(t * P, (t + 1) * P)
                            three_pass(nc, psum[:, n % BANKS, 0:DM],
                                       [((xh[:, k, cols], xl[:, k, cols]), (wh[2][:, k, :], wl[2][:, k, :]))
                                        for k in range(KC)]).then_inc(product, 1)

                @block.scalar
                def _(act):
                    for n, (w, c, t) in enumerate(items):
                        if w == 2:
                            continue
                        high = dst[w][0]
                        part = high[:, 2 * (t // 2) + c, 512 * (t % 2):512 * (t % 2) + 512]
                        act.wait_ge(product, n + 1)
                        nc.scalar.activation(part.bitcast(FP32R), psum[:, n % BANKS, :], ACT.Copy)\
                            .then_inc(high_ready, 1)

                @block.vector
                def _(dve):
                    for w in range(3):
                        dve.wait_ge(loaded[w], 16)
                        nc.vector.tensor_copy(wh[w][:, :, :], raw[w][:, :, :]).then_inc(v_seq, 1)
                        dve.wait_ge(v_seq, w + 1)
                        nc.vector.tensor_tensor(wl[w][:, :, :], raw[w][:, :, :], wh[w][:, :, :],
                                                ALU.subtract).then_inc(split, 1)
                    for n, (w, c, t) in enumerate(items):
                        if w == 2:
                            dve.wait_ge(product, n + 1)
                            nc.vector.tensor_copy(v0[:, t, :], psum[:, n % BANKS, 0:DM]).then_inc(bank_free, 1)
                            continue
                        high, low = dst[w]
                        at = (slice(None), 2 * (t // 2) + c, slice(512 * (t % 2), 512 * (t % 2) + 512))
                        dve.wait_ge(high_ready, n + 1)
                        nc.vector.tensor_tensor(low[at].bitcast(FP32R), psum[:, n % BANKS, :], high[at],
                                                ALU.subtract).then_inc(bank_free, 1)


        QUAD = 4
        TURNS = BATCH * H0 // (2 * QUAD)
        with ExitStack() as ctx:
            sb = lambda n, s, d=FP32: ctx.enter_context(nc.sbuf_tensor(f"s0_{n}", s, d))
            sem = lambda n: ctx.enter_context(nc.semaphore(f"s0_{n}"))
            q3 = [sb(f"q3_{n}", [P, QUAD, SEQ], FP32R) for n in range(2)]
            k3 = [sb(f"k3_{n}", [P, QUAD, SEQ], FP32R) for n in range(2)]
            probs = sb("probs", [P, 2, QUAD, SEQ])
            values = [sb(f"values{n}", [P, NB, QUAD, 32]) for n in range(2)]
            part_max = sb("part_max", [P, QUAD, NB, 2])
            neg_max = sb("neg_max", [P, QUAD * NB])
            max_high, max_low = sb("max_high", [QUAD * NB, P], FP32R), sb("max_low", [QUAD * NB, P], FP32R)
            out_sb = sb("out_sb", [P, SEQ])
            recip = sb("recip", [P, 4, QUAD])
            loaded = [[sem(f"loaded{q}{h}") for h in range(2)] for q in range(2)]
            (max_rows, values_ready, small_filled, small_free, scores_ready, exps_done, pvs_done, outs_copied,
             neg_ready, high_done, recip_done, setup, ones_set) = map(sem, (
                 "max_rows", "values_ready", "small_filled", "small_free", "scores_ready", "exps_done",
                 "pvs_done", "outs_copied", "neg_ready", "high_done", "recip_done", "setup",
                 "ones_set"))
            flat = psum[:, :, :].rearrange("p a b -> p (a b)")
            OUT = 4 * 512
            small_bank = lambda n: 6 + n % 2
            qh_flat = qh[:, :, :].rearrange("p t d -> p (t d)")
            v0_flat = v0[:, :, :].rearrange("p t d -> p (t d)")

            SEGS = [(qb, h, s, min(512, P * (qb + 1) - 512 * s))
                    for qb in range(NB) for h in range(QUAD) for s in range(1 + qb // 4)]
            STEPS = [(kb, h) for kb in range(NB) for h in range(QUAD)]

            def plan(outputs_too, n):
                steps = [[("max", s) for s in range(2 * t, min(2 * t + 2, len(SEGS)))] for t in range(len(STEPS))]
                steps[len(SEGS) // 2 + 1].append(("turn", 0))
                if outputs_too:
                    steps[2].append(("out", 0))
                    steps[3].append(("out", 1))
                numbered = []
                for step in steps:
                    numbered.append([(n + i, kind, arg) for i, (kind, arg) in enumerate(step)])
                    n += len(step)
                return numbered, n

            AHEAD = len(SEGS) + 1
            plan_a, n_b = plan(False, AHEAD)
            plan_b, n_tail = plan(True, n_b)
            PLANS = [plan_a, plan_b]
            TAIL = [(n_tail, "out", 0), (n_tail + 1, "out", 1)]
            PER = n_tail + 2 - AHEAD
            assert PER % 2 == 0
            FIRST = [(n, "max", n) for n in range(len(SEGS))] + [(len(SEGS), "turn", 0)]
            FAR_SEG = min(n for n, seg in enumerate(SEGS) if seg[0] == 4)
            OUT_ITEM = [n for step in plan_b for n, kind, arg in step if (kind, arg) == ("out", 1)][0]
            TURN_ITEM = [n for p in PLANS for step in p for n, kind, _ in step if kind == "turn"]
            NT = len(STEPS)
            LOAD = 16 * 25

            with nc.Block() as block:
                @block.sync
                def _(sp):
                    def load(quad, half, slot):
                        cols = slice(512 * half, 512 * half + 512)
                        for to, high, low, order in ((q3[quad], qh, ql, (0, 1, 0)), (k3[quad], kh, kl, (0, 0, 1))):
                            for row, part in enumerate(order):
                                for h in range(QUAD):
                                    first = 64 * quad + 16 * h
                                    sp.dma_start(to[16 * row:16 * row + 16, h:h + 1, cols].bitcast(FP32),
                                                 (high, low)[part][first:first + 16, bass.ds(slot, 1), cols])\
                                        .then_inc(loaded[quad][half], 16)
                        sp.dma_start(q3[quad][48:50, :, cols].bitcast(FP32), q3[quad][100:102, :, cols].bitcast(FP32))\
                            .then_inc(loaded[quad][half], 16)

                    def put_max(quad, turn_item):
                        sp.wait_ge(small_free, turn_item + 3)
                        for row, part in ((48, max_high), (49, max_low)):
                            sp.dma_start(q3[quad][row:row + 1, :, :].rearrange("o h n -> o (h n)").bitcast(FP32),
                                         part[:, :].bitcast(FP32)).then_inc(max_rows, 16)

                    sp.wait_ge(setup, 7)
                    for quad in range(2):
                        for half in range(2):
                            load(quad, half, 0)
                    put_max(0, AHEAD - 1)
                    with sp.Fori(0, TURNS, 1) as j:
                        for quad in range(2):
                            sp.wait_ge(scores_ready, j * (2 * NT) + NT * quad + NT // 2)
                            load(quad, 0, (j + 1) % TURNS)
                            put_max(1 - quad, j * PER + TURN_ITEM[quad])
                            sp.wait_ge(scores_ready, j * (2 * NT) + NT * quad + NT)
                            load(quad, 1, (j + 1) % TURNS)
                    for quad in range(2):
                        for half in range(2):
                            sp.wait_ge(loaded[quad][half], LOAD * (TURNS + 1))
                    sp.wait_ge(max_rows, 32 * (2 * TURNS + 1))

                @block.gpsimd
                def _(pool):
                    def gather(quad, slot):
                        for kb in range(NB):
                            src = v0_flat[:, bass.ds((slot // 2) * (NB * DM) + (slot % 2) * P + kb * DM + 64 * quad, 64)]
                            last = nc.gpsimd.tensor_copy(values[quad][:, kb, :, 0:HD0],
                                                         src.rearrange("p (h d) -> p h d", h=QUAD))
                        last.then_inc(values_ready, 1)

                    for n in range(2):
                        nc.gpsimd.memset(q3[n][:, :, :].bitcast(FP32), 0.0).then_inc(setup, 1)
                        nc.gpsimd.memset(k3[n][:, :, :].bitcast(FP32), 1.0).then_inc(setup, 1)
                    pool.wait_ge(ones_set, 2)
                    gather(0, 0)
                    gather(1, 0)
                    with pool.Fori(0, TURNS, 1) as j:
                        for quad in range(2):
                            pool.wait_ge(pvs_done, j * (2 * NB) + NB * quad + NB + 2)
                            gather(quad, (j + 1) % TURNS)

                @block.vector
                def _(dve):
                    nc.vector.memset(part_max[:, :, :, :], LOWEST).then_inc(setup, 1)
                    for n in range(2):
                        nc.vector.memset(values[n][:, :, :, :], 0.0).then_inc(setup, 1)
                    dve.wait_ge(setup, 7)
                    for n in range(2):
                        nc.vector.memset(values[n][:, :, :, HD0:HD0 + 1], 1.0).then_inc(ones_set, 1)

                    def small(j, n, kind, arg, quad, nth):
                        done = n if j is None else j * PER + n
                        bank = psum[:, small_bank(n), :]
                        if kind != "max":
                            dve.wait_ge(small_free, done + 2)
                        if kind == "turn":
                            nc.vector.tensor_reduce(
                                neg_max[:, :], part_max[:, :, :, :].rearrange("p h b s -> p (h b) s"),
                                axis=AXIS.X, op=ALU.max, negate=True).then_inc(neg_ready, 1)
                        dve.wait_ge(small_filled, done + 1)
                        if kind == "max":
                            qb, h, s, width = SEGS[arg]
                            nc.vector.reduce_max(part_max[:, h, qb, s:s + 1], bank[:, 0:width], AXIS.X)\
                                .then_inc(small_free, 1)
                        elif kind == "turn":
                            if j is not None:
                                dve.wait_ge(max_rows, nth * 32)
                            nc.vector.tensor_copy(max_high[:, :], bank[0:QUAD * NB, 0:P]).then_inc(high_done, 1)
                            dve.wait_ge(high_done, nth + 1)
                            nc.vector.tensor_tensor(max_low[:, :], bank[0:QUAD * NB, 0:P], max_high[:, :],
                                                    ALU.subtract).then_inc(small_free, 1)
                        else:
                            view = bank.rearrange("p (b h d) -> p b h d", b=4, h=QUAD)
                            nc.vector.reciprocal(recip[:, :, :], view[:, :, :, HD0]).then_inc(recip_done, 1)
                            dve.wait_ge(recip_done, nth + 1)
                            for b in range(4):
                                to = qh_flat[:, bass.ds(j * SEQ + (P * (4 * arg + b) + 64 * quad), 64)]
                                last = nc.vector.tensor_tensor(
                                    to.rearrange("p (h d) -> p h d", h=QUAD), view[:, b, :, 0:HD0],
                                    recip[:, b, :].unsqueeze(2).broadcast_to([P, QUAD, HD0]), ALU.mult)
                            last.then_inc(small_free, 1)

                    for n, kind, arg in FIRST:
                        small(None, n, kind, arg, 0, 0)
                    with dve.Fori(0, TURNS, 1) as j:
                        for quad in range(2):
                            for step in PLANS[quad]:
                                for n, kind, arg in step:
                                    if kind == "out":
                                        small(j, n, kind, arg, 0, j * 4 + arg)
                                    else:
                                        small(j, n, kind, arg, 1 - quad, j * 2 + (quad + 1))
                        for n, kind, arg in TAIL:
                            small(j, n, kind, arg, 1, j * 4 + (2 + arg))

                @block.scalar
                def _(act):
                    act.sem_inc(exps_done, 2)
                    act.sem_inc(outs_copied, 1)
                    with act.Fori(0, TURNS, 1) as j:
                        for quad in range(2):
                            for t, (kb, h) in enumerate(STEPS):
                                act.wait_ge(scores_ready, j * (2 * NT) + (NT * quad + t + 1))
                                if h == 0:
                                    act.wait_ge(pvs_done, j * (2 * NB) + (NB * quad + kb + 1))
                                buf = 1024 * (t % 2)
                                nc.scalar.activation(probs[:, kb % 2, h, kb * P:SEQ], flat[:, buf + kb * P:buf + SEQ],
                                                     ACT.Exp, scale=HD0 ** -0.5).then_inc(exps_done, 1)
                            act.wait_ge(pvs_done, j * (2 * NB) + (NB * quad + NB + 2))
                            read = AHEAD if quad == 0 else OUT_ITEM + 1
                            act.wait_ge(small_filled, j * PER + read)
                            nc.scalar.activation(out_sb[:, :], flat[:, OUT:OUT + SEQ], ACT.Copy)\
                                .then_inc(outs_copied, 1)

                @block.tensor
                def _(pe):
                    pe.sem_inc(small_free, 2)
                    pe.sem_inc(pvs_done, 2)

                    def small(j, n, kind, arg, quad, nth):
                        done = n if j is None else j * PER + n
                        bank = psum[:, small_bank(n), :]
                        pe.wait_ge(small_free, done + 1)
                        if kind == "max":
                            qb, h, s, width = SEGS[arg]
                            if arg in (0, FAR_SEG):
                                half = int(arg > 0)
                                pe.wait_ge(loaded[quad][half], nth * LOAD)
                            diagonal = s == qb // 4
                            last = nc.tensor.matmul(bank[:, 0:width], q3[quad][:, h, qb * P:qb * P + P],
                                                    k3[quad][:, h, 512 * s:512 * s + width], start=True,
                                                    stop=not diagonal)
                            if diagonal:
                                last = nc.tensor.matmul(bank[:, width - P:width], ident_b[:, :], mask_q[:, :],
                                                        start=False, stop=True)
                        elif kind == "turn":
                            pe.wait_ge(neg_ready, nth)
                            last = nc.tensor.transpose(bank[0:QUAD * NB, 0:P], neg_max[:, :], ident[:, :])
                        else:
                            pe.wait_ge(outs_copied, nth)
                            for b in range(4):
                                at = (4 * arg + b) * P
                                last = nc.tensor.transpose(bank[:, b * P:b * P + P], out_sb[:, at:at + P], ident[:, :])
                        last.then_inc(small_filled, 1)

                    def scores(j, quad, t, kb, h):
                        pe.wait_ge(exps_done, j * (2 * NT) + (NT * quad + t + 1))
                        buf = 1024 * (t % 2)
                        keys = k3[quad][:, h, kb * P:kb * P + P]
                        for q0, q1 in ((kb * P, 512), (max(kb * P, 512), SEQ)):
                            if q0 >= q1:
                                continue
                            diagonal = q0 == kb * P
                            last = nc.tensor.matmul(flat[:, buf + q0:buf + q1], keys, q3[quad][:, h, q0:q1],
                                                    start=True, stop=not diagonal)
                            if diagonal:
                                last = nc.tensor.matmul(flat[:, buf + q0:buf + q0 + P], ident_b[:, :], mask_k[:, :],
                                                        start=False, stop=True)
                        last.then_inc(scores_ready, 1)

                    def mix(j, quad, kb):
                        pe.wait_ge(exps_done, j * (2 * NT) + (NT * quad + QUAD * (kb + 1) + 2))
                        if kb == 0:
                            pe.wait_ge(outs_copied, j * 2 + (quad + 1))
                            pe.wait_ge(values_ready, j * 2 + (quad + 1))
                        for q0, q1 in ((kb * P, 512), (max(kb * P, 512), SEQ)):
                            if q0 >= q1:
                                continue
                            for h in range(QUAD):
                                last = nc.tensor.matmul(flat[32 * h:32 * h + 32, OUT + q0:OUT + q1],
                                                        values[quad][:, kb, h, :], probs[:, kb % 2, h, q0:q1],
                                                        start=(kb == 0), stop=(kb == (3 if q1 == 512 else NB - 1)))
                        last.then_inc(pvs_done, 1)

                    for n, kind, arg in FIRST:
                        small(None, n, kind, arg, 0, 1)
                    with pe.Fori(0, TURNS, 1) as j:
                        for quad in range(2):
                            for t, (kb, h) in enumerate(STEPS):
                                if t == 0:
                                    pe.wait_ge(max_rows, j * 64 + 32 * (quad + 1))
                                scores(j, quad, t, kb, h)
                                for n, kind, arg in PLANS[quad][t]:
                                    nth = {"max": j + (quad + 1), "turn": j * 2 + (quad + 2), "out": j * 2 + 2}[kind]
                                    small(j, n, kind, arg, 1 - quad, nth)
                                if h == 1 and kb > 0:
                                    mix(j, quad, kb - 1)
                            mix(j, quad, NB - 1)
                        for n, kind, arg in TAIL:
                            small(j, n, kind, arg, 1, j * 2 + 3)

        with ExitStack() as ctx:
            sb = lambda n, s, d=FP32: ctx.enter_context(nc.sbuf_tensor(f"o0_{n}", s, d))
            sem = lambda n: ctx.enter_context(nc.semaphore(f"o0_{n}"))
            weights = sb("weights", [P, KC, DM])
            turned_sb = sb("turned", [P, 2, KC * P])
            loaded, turned, copied, product, added = map(sem, ("loaded", "turned", "copied", "product", "added"))
            with nc.Block() as block:
                @block.sync
                def _(sp):
                    sp.dma_start(weights[:, :, :], wo0).then_inc(loaded, 16)

                @block.tensor
                def _(pe):
                    pe.wait_ge(loaded, 16)

                    def turn(t):
                        if t >= 2:
                            pe.wait_ge(copied, t - 1)
                        b, qb = divmod(t, NB)
                        for c in range(KC):
                            last = nc.tensor.transpose(psum[:, t % 2, c * P:c * P + P],
                                                       qh[:, 2 * b + c, qb * P:qb * P + P], ident[:, :])
                        last.then_inc(turned, 1)

                    turn(0)
                    for t in range(TT):
                        if t + 1 < TT:
                            turn(t + 1)
                        pe.wait_ge(copied, t + 1)
                        if t >= 2:
                            pe.wait_ge(added, t - 1)
                        for c in range(KC):
                            last = nc.tensor.matmul(psum[:, 2 + t % 2, 0:DM], turned_sb[:, t % 2, c * P:c * P + P],
                                                    weights[:, c, :], start=(c == 0), stop=(c == KC - 1))
                        last.then_inc(product, 1)

                @block.scalar
                def _(act):
                    for t in range(TT):
                        act.wait_ge(turned, t + 1)
                        if t >= 2:
                            act.wait_ge(product, t - 1)
                        nc.scalar.activation(turned_sb[:, t % 2, :], psum[:, t % 2, 0:KC * P], ACT.Copy)\
                            .then_inc(copied, 1)

                @block.vector
                def _(dve):
                    for t in range(TT):
                        dve.wait_ge(product, t + 1)
                        nc.vector.tensor_tensor(x[:, t, :], psum[:, 2 + t % 2, 0:DM], x[:, t, :], ALU.add)\
                            .then_inc(added, 1)


def ternary_ffn(nc, x, ident, psum, w1, w3, w2):
    with ExitStack() as ctx:
        sb = lambda n, s, d=FP32: ctx.enter_context(nc.sbuf_tensor(f"f0_{n}", s, d))
        sem = lambda n: ctx.enter_context(nc.semaphore(f"f0_{n}"))
        xh, xl = sb("xh", [P, KC, TOK], FP32R), sb("xl", [P, KC, TOK], FP32R)
        layer_norm(nc, "n1", x, xh, xl, ident, psum)
        raw = [sb("raw1", [P, KC, HC * P]), sb("raw3", [P, KC, HC * P]), sb("raw2", [P, HC, DM])]
        below = sb("below", [P, HC * DM])
        signs = [sb("signs1", [P, KC, HC * P], FP32R), sb("signs3", [P, KC, HC * P], FP32R), sb("signs2", [P, HC, DM])]
        sums = sb("sums", [P, 3])
        scales = sb("scales", [P, 3])
        half, minus_half = sb("half", [P, 3]), sb("minus_half", [P, 3])
        scale_out = sb("scale_out", [P, 1])
        ones = sb("ones", [P, P])
        gate = sb("gate", [P, 2, 512])
        hidden = sb("hidden", [P, HC, 512])
        loaded = [sem(f"loaded{n}") for n in range(3)]
        (v_seq, summed, totals, signs_ready, up_ready, gates_done, hidden_done, out_ready, added) = map(sem, (
            "v_seq", "summed", "totals", "signs_ready", "up_ready", "gates_done", "hidden_done", "out_ready",
            "added"))
        BLOCKS = TOK // 512
        UP, OUT = (0, 2), 4

        with nc.Block() as block:
            @block.sync
            def _(sp):
                for n, w in enumerate((w1, w3, w2)):
                    sp.dma_start(raw[n][:, :, :], w).then_inc(loaded[n], 16)

            @block.vector
            def _(dve):
                v = Chain(dve, v_seq)
                v.link(nc.vector.memset(ones[:, :], 1.0))
                for n in range(3):
                    dve.wait_ge(loaded[n], 16)
                    last = nc.vector.tensor_reduce(sums[:, n:n + 1], raw[n][:, :, :], axis=AXIS.XY, op=ALU.add,
                                                   apply_absolute_value=True)
                last.then_inc(summed, 1)
                dve.wait_ge(totals, 1)
                v.link(nc.vector.tensor_scalar(scales[:, :], psum[:, 7, 0:3], 1.0 / (HID * DM), None, ALU.mult))
                v.link(nc.vector.tensor_scalar(half[:, :], scales[:, :], 0.5, None, ALU.mult))
                v.link(nc.vector.tensor_scalar(minus_half[:, :], scales[:, :], -0.5, None, ALU.mult))
                v.link(nc.vector.tensor_tensor(scale_out[:, :], scales[:, 1:2], scales[:, 2:3], ALU.mult))
                for n in range(3):
                    flat_raw = raw[n][:, :, :].rearrange("p a b -> p (a b)")
                    flat_signs = signs[n][:, :, :].rearrange("p a b -> p (a b)")
                    v.link(nc.vector.tensor_scalar(below[:, :], flat_raw, minus_half[:, n:n + 1], None, ALU.is_lt))
                    nc.vector.scalar_tensor_tensor(flat_signs, flat_raw, half[:, n:n + 1], below[:, :], ALU.is_gt,
                                                   ALU.subtract).then_inc(signs_ready, 1)
                    dve.wait_ge(signs_ready, n + 1)
                with dve.Fori(0, BLOCKS, 1) as i:
                    for c in range(HC):
                        dve.wait_ge(gates_done, i * HC + (c + 1))
                        nc.vector.tensor_tensor(hidden[:, c, :], psum[:, UP[1] + c % 2, :], gate[:, c % 2, :],
                                                ALU.mult).then_inc(hidden_done, 1)
                    for t in range(4):
                        dve.wait_ge(out_ready, i * 4 + (t + 1))
                        rows = x[:, bass.ds(i * 4 + t, 1), :]
                        nc.vector.scalar_tensor_tensor(rows, psum[:, OUT + t:OUT + t + 1, 0:DM], scale_out[:, :], rows,
                                                       ALU.mult, ALU.add).then_inc(added, 1)

            @block.scalar
            def _(act):
                act.wait_ge(signs_ready, 1)
                with act.Fori(0, BLOCKS, 1) as i:
                    for c in range(HC):
                        act.wait_ge(up_ready, i * HC + (c + 1))
                        act.wait_ge(hidden_done, i * HC + (c + 1))
                        nc.scalar.activation(gate[:, c % 2, :], psum[:, UP[0] + c % 2, :], ACT.Silu,
                                             scale=scales[:, 0:1]).then_inc(gates_done, 1)

            @block.tensor
            def _(pe):
                pe.sem_inc(hidden_done, 2)
                pe.sem_inc(added, 4)
                pe.wait_ge(summed, 1)
                nc.tensor.matmul(psum[:, 7, 0:3], ones[:, :], sums[:, :], start=True, stop=True).then_inc(totals, 1)
                pe.wait_ge(signs_ready, 3)
                with pe.Fori(0, BLOCKS, 1) as i:
                    for c in range(HC):
                        pe.wait_ge(hidden_done, i * HC + (c + 1))
                        for w in range(2):
                            n = 0
                            for k in range(KC):
                                for part in (xh, xl):
                                    last = nc.tensor.matmul(psum[:, UP[w] + c % 2, :],
                                                            signs[w][:, k, c * P:c * P + P],
                                                            part[:, k, bass.ds(i * 512, 512)],
                                                            start=(n == 0), stop=(n == 2 * KC - 1))
                                    n += 1
                        last.then_inc(up_ready, 1)
                    pe.wait_ge(hidden_done, i * HC + (HC + 2))
                    for t in range(4):
                        pe.wait_ge(added, i * 4 + (t + 1))
                        for c in range(HC):
                            last = nc.tensor.matmul(psum[:, OUT + t, 0:DM], hidden[:, c, t * P:t * P + P],
                                                    signs[2][:, c, :], start=(c == 0), stop=(c == HC - 1))
                        last.then_inc(out_ready, 1)


def layer1_attention(nc, x, ident, keep, psum, wqk1, wv1, wo1, bo1, aux, key_aux, cosines, sines):
    with ExitStack() as ctx:
        sb = lambda n, s, d=FP32: ctx.enter_context(nc.sbuf_tensor(f"a1_{n}", s, d))
        xh, xl = sb("xh", [P, KC, TOK], FP32R), sb("xl", [P, KC, TOK], FP32R)
        layer_norm(nc, "n2", x, xh, xl, ident, psum)
        v_dram = nc.dram_tensor("v_scratch", [TT, P, G1 * HD1], FP32).ap()
        aux_dram = nc.dram_tensor("aux_scratch", [G1 * AUX, REP * SEQ], FP32).ap()

        with ExitStack() as prep:
            tb = lambda n, s, d=FP32: prep.enter_context(nc.sbuf_tensor(f"v1_{n}", s, d))
            sem = lambda n: prep.enter_context(nc.semaphore(f"v1_{n}"))
            raw = tb("raw", [P, KC, G1 * HD1])
            wh, wl = tb("wh", [P, KC, G1 * HD1], FP32R), tb("wl", [P, KC, G1 * HD1], FP32R)
            staged = tb("staged", [P, 4, G1 * HD1])
            aux_raw = tb("aux_raw", [G1 * AUX, REP * SEQ])
            aux_r = tb("aux_r", [G1 * AUX, REP * SEQ], FP32R)
            bias = tb("bias", [P, DM])
            w_loaded, a_loaded, b_loaded, split, v_seq, product, copied, a_done = map(
                sem, ("w_loaded", "a_loaded", "b_loaded", "split", "v_seq", "product", "copied", "a_done"))
            stored = [sem(f"stored{n}") for n in range(4)]
            a_stored = sem("a_stored")
            with nc.Block() as block:
                @block.sync
                def _(sp):
                    sp.dma_start(raw[:, :, :], wv1).then_inc(w_loaded, 16)
                    sp.dma_start(aux_raw[:, :], aux).then_inc(a_loaded, 16)
                    sp.dma_start(bias[:, :], bo1.partition_broadcast(P)).then_inc(b_loaded, 16)
                    for t in range(TT):
                        sp.wait_ge(copied, t + 1)
                        sp.dma_start(v_dram[t, :, :], staged[:, t % 4, :]).then_inc(stored[t % 4], 16)
                    sp.wait_ge(a_done, 1)
                    sp.dma_start(aux_dram, aux_r[:, :].bitcast(FP32)).then_inc(a_stored, 16)
                    sp.wait_ge(a_stored, 16)
                    for n in range(4):
                        sp.wait_ge(stored[n], 16 * (TT // 4))

                @block.vector
                def _(dve):
                    dve.wait_ge(w_loaded, 16)
                    nc.vector.tensor_copy(wh[:, :, :], raw[:, :, :]).then_inc(v_seq, 1)
                    dve.wait_ge(v_seq, 1)
                    nc.vector.tensor_tensor(wl[:, :, :], raw[:, :, :], wh[:, :, :], ALU.subtract).then_inc(split, 1)
                    dve.wait_ge(a_loaded, 16)
                    nc.vector.tensor_copy(aux_r[:, :], aux_raw[:, :]).then_inc(a_done, 1)
                    dve.wait_ge(b_loaded, 16)
                    for t in range(TT):
                        last = nc.vector.tensor_tensor(x[:, t, :], x[:, t, :], bias[:, :], ALU.add)
                    last.then_inc(v_seq, 1)

                @block.tensor
                def _(pe):
                    pe.wait_ge(split, 1)
                    for t in range(TT):
                        if t >= 4:
                            pe.wait_ge(copied, t - 3)
                        cols = slice(t * P, t * P + P)
                        three_pass(nc, psum[:, t % 4, :], [((xh[:, k, cols], xl[:, k, cols]), (wh[:, k, :], wl[:, k, :]))
                                                           for k in range(KC)]).then_inc(product, 1)

                @block.scalar
                def _(act):
                    for t in range(TT):
                        act.wait_ge(product, t + 1)
                        if t >= 4:
                            act.wait_ge(stored[t % 4], 16 * (t // 4))
                        nc.scalar.activation(staged[:, t % 4, :], psum[:, t % 4, :], ACT.Copy).then_inc(copied, 1)

        sem = lambda n: ctx.enter_context(nc.semaphore(f"a1_{n}"))
        queries = [sb(f"queries{b}", [P, 2, REP, SEQ], FP32R) for b in range(BATCH)]
        keys_hh = [sb(f"keys_hh{b}", [P, SEQ], FP32R) for b in range(BATCH)]
        keys_la = [sb(f"keys_la{b}", [P, SEQ], FP32R) for b in range(BATCH)]
        values = [sb(f"values{b}", [P, NB, HD1]) for b in range(BATCH)]
        probs = sb("probs", [P, 2, 2, SEQ])
        cos_sb, sin_sb = sb("cos", [P, SEQ]), sb("sin", [P, SEQ])
        straight, swapped = sb("straight", [P, 2, 512]), sb("swapped", [P, 2, 512])
        high, low = sb("high", [P, 2, 512], FP32R), sb("low", [P, 2, 512], FP32R)
        out_sb, den_sb = sb("out_sb", [P, SEQ]), sb("den_sb", [P, 512])
        recip = sb("recip", [P, NB, 2])
        context = sb("context", [P, NB, P])
        context_t = [sb(f"context_t{p}", [P, SEQ]) for p in range(2)]
        w_raw = sb("w_raw", [P, KC, (REP + 1) * HD1])
        wq_h, wq_l = sb("wq_h", [P, KC, REP * HD1], FP32R), sb("wq_l", [P, KC, REP * HD1], FP32R)
        wk_h, wk_l = sb("wk_h", [P, KC, 2, HD1], FP32R), sb("wk_l", [P, KC, 2, HD1], FP32R)
        wo_sb = sb("wo_sb", [P, 2, DM])
        ones = sb("ones", [P, 32])
        (w_loaded, w_split, wh_done, tables, wo_loaded, work_filled, work_free, scores_ready, tanhs_done, exps_done,
         masks_done, mixes_done, outs_free, turned, roped, split_done, high_done, setup, key_aux_in, p_seq) = map(sem, (
             "w_loaded", "w_split", "wh_done", "tables", "wo_loaded", "work_filled", "work_free", "scores_ready",
             "tanhs_done", "exps_done", "masks_done", "mixes_done", "outs_free", "turned", "roped", "split_done",
             "high_done", "setup", "key_aux_in", "p_seq"))
        zeros_set = sem("zeros_set")
        placed = [sem(f"placed{n}") for n in range(2)]
        aux_loaded = [sem(f"aux_loaded{b}") for b in range(BATCH)]
        v_loaded = [sem(f"v_loaded{b}") for b in range(BATCH)]
        flat = psum[:, :, :].rearrange("p a b -> p (a b)")
        OUT, DEN, WORK = 4 * 512, 6, 7
        STEPS = 2 * NB
        NT = 2 * STEPS

        def plan(unit, n):
            steps = [[] for _ in range(STEPS)]
            nxt = 1 - unit
            for i, it in enumerate([("q", nxt, p, h) for p in range(2) for h in range(2)] + [("k", nxt, None, h) for h in range(2)]):
                steps[i].append(it)
            end = [("den",), ("ctx", 0), ("ctx", 1), ("back", 0), ("back", 1)]
            for i, it in enumerate(end):
                steps[1 + i].append(it + (1, 1 - unit)[-2:])
                steps[NB + 1 + i].append(it + (0, unit)[-2:])
            for i in range(4):
                steps[6 + i // 2].append(("wo", i, None, 1 - unit))
            numbered = []
            for step in steps:
                numbered.append([(n + i, it) for i, it in enumerate(step)])
                n += len(step)
            return numbered, n

        FIRST = [(i, it) for i, it in enumerate([("q", 0, p, h) for p in range(2) for h in range(2)] +
                                                [("k", 0, None, h) for h in range(2)])]
        plan0, n1 = plan(0, len(FIRST))
        plan1, n2 = plan(1, n1)
        PLANS, PER = [plan0, plan1], n2 - len(FIRST)
        LAST = [(n2, ("den", 1, 1)), (n2 + 1, ("ctx", 0, 1, 1)), (n2 + 2, ("ctx", 1, 1, 1)),
                (n2 + 3, ("back", 0, 1, 1)), (n2 + 4, ("back", 1, 1, 1))] + \
               [(n2 + 5 + i, ("wo", i, None, 1)) for i in range(4)]
        WO_ITEM = [n for step in plan0 for n, it in step if it[0] == "wo"][-1]
        ROPES = len(FIRST)
        SPLIT_W = NB

        def ropes(u):
            out, r = [], 0
            for step in PLANS[u]:
                row = [it for _, it in step if it[0] in "qk"]
                out.append([(r + i, it) for i, it in enumerate(row)])
                r += len(row)
            return out

        with nc.Block() as block:
            @block.sync
            def _(sp):
                def load_w(g):
                    sp.dma_start(w_raw[:, :, :], wqk1[bass.ds(g, 1), :, :].rearrange("o p (k n) -> p (o k) n", k=KC))\
                        .then_inc(w_loaded, 16)

                def load_aux(b, g):
                    sp.dma_start(queries[b][64:64 + AUX, 1, :, :].rearrange("p h n -> p (h n)").bitcast(FP32),
                                 aux_dram[bass.ds(g * AUX, AUX), :]).then_inc(aux_loaded[b], 16)

                def load_v(b, g):
                    sp.dma_start(values[b][:, :, :],
                                 v_dram[b * NB:b * NB + NB, :, bass.ds(g * HD1, HD1)].rearrange("t p d -> p t d"))\
                        .then_inc(v_loaded[b], 16)

                def load_wo(g):
                    sp.dma_start(wo_sb[:, :, :], wo1[bass.ds(g, 1), :, :].rearrange("o p (k n) -> p (o k) n", k=2))\
                        .then_inc(wo_loaded, 16)

                def place(r, it):
                    _, b, p, h = it
                    s = p * 2 + h
                    sp.wait_ge(split_done, r)
                    cols = slice(h * 512, h * 512 + 512)
                    for a in range(2):
                        rows = slice(64 * a, 64 * a + 64)
                        sp.dma_start(queries[b][0:64, :, 2 * p + a, cols].bitcast(FP32),
                                     high[rows, s % 2, :].bitcast(FP32).unsqueeze(1).broadcast_to([64, 2, 512]))\
                            .then_inc(placed[s % 2], 16)
                        sp.dma_start(queries[b][64:128, 0, 2 * p + a, cols].bitcast(FP32),
                                     low[rows, s % 2, :].bitcast(FP32)).then_inc(placed[s % 2], 16)

                load_w(0)
                sp.dma_start(cos_sb[:, :], cosines).then_inc(tables, 16)
                sp.dma_start(sin_sb[:, :], sines).then_inc(tables, 16)
                sp.dma_start(out_sb[64:128, :], key_aux).then_inc(key_aux_in, 16)
                load_wo(0)
                sp.wait_ge(zeros_set, 2)
                for b in range(BATCH):
                    load_aux(b, 0)
                    load_v(b, 0)
                sp.wait_ge(w_split, 1)
                load_w(1)
                for r, (_, it) in enumerate(FIRST):
                    if it[0] == "q":
                        place(r + 1, it)
                with sp.Fori(0, G1, 1) as g:
                    for u in range(2):
                        for step in ropes(u):
                            for r, it in step:
                                if it[0] == "q":
                                    place(g * (2 * ROPES) + (ROPES * (u + 1) + r + 1), it)
                        if u == 0:
                            sp.wait_ge(work_filled, g * PER + (WO_ITEM + 1))
                            load_wo(g)
                            sp.wait_ge(w_split, g + 2)
                            load_w((g + 2) % G1)
                        sp.wait_ge(scores_ready, g * (2 * NT) + NT * (u + 1))
                        load_aux(u, (g + 1) % G1)
                        sp.wait_ge(mixes_done, g * (2 * STEPS) + (STEPS * (u + 1) + 2))
                        load_v(u, (g + 1) % G1)
                sp.wait_ge(w_loaded, 16 * (G1 + 2))
                for b in range(BATCH):
                    sp.wait_ge(aux_loaded[b], 16 * (G1 + 1))
                    sp.wait_ge(v_loaded[b], 16 * (G1 + 1))
                for n in range(2):
                    sp.wait_ge(placed[n], 128 * (2 * G1 + 1))

            @block.gpsimd
            def _(pool):
                for b in range(BATCH):
                    nc.gpsimd.memset(queries[b][64:128, 1, :, :].bitcast(FP32), 0.0).then_inc(zeros_set, 1)

                def rope(r, item_done, slot, it):
                    h = it[3]
                    pool.wait_ge(work_free, item_done)
                    nc.gpsimd.tensor_tensor(swapped[:, slot, :], swapped[:, slot, :], sin_sb[:, h * 512:h * 512 + 512],
                                            ALU.mult).then_inc(p_seq, 1)
                    pool.wait_ge(p_seq, r)
                    nc.gpsimd.tensor_tensor(straight[:, slot, :], straight[:, slot, :], swapped[:, slot, :],
                                            ALU.add).then_inc(roped, 1)

                pool.wait_ge(tables, 32)
                for r, (n, it) in enumerate(FIRST):
                    rope(r + 1, n + 2, r % 2, it)
                with pool.Fori(0, G1, 1) as g:
                    for u in range(2):
                        rows = ropes(u)
                        for s in range(STEPS):
                            for n, it in PLANS[u][s]:
                                if it[0] in "qk":
                                    r = rows[s][0][0]
                                    rope(g * (2 * ROPES) + (ROPES * (u + 1) + r + 1), g * PER + (n + 2), r % 2, it)
                            pool.wait_ge(exps_done, g * (2 * NT) + (NT * u + 2 * s + 2 + 2))
                            kb = s % NB
                            part = probs[:, s % 2, :, kb * P:kb * P + P]
                            nc.gpsimd.tensor_tensor(part, part, keep[:, :].unsqueeze(1).broadcast_to([P, 2, P]),
                                                    ALU.mult).then_inc(masks_done, 1)

            @block.scalar
            def _(act):
                act.sem_inc(exps_done, 2)
                with act.Fori(0, G1, 1) as g:
                    for u in range(2):
                        def tanh(t):
                            kb = (t // 2) % NB
                            part = flat[:, 1024 * (t % 2) + kb * P:1024 * (t % 2) + SEQ]
                            act.wait_ge(scores_ready, g * (2 * NT) + (NT * u + t + 1))
                            nc.scalar.activation(part, part, ACT.Tanh, scale=1.0 / (30.0 * HD1 ** 0.5))\
                                .then_inc(tanhs_done, 1)

                        tanh(0)
                        for t in range(NT):
                            if t + 1 < NT:
                                tanh(t + 1)
                            kb, s = (t // 2) % NB, t // 2
                            act.wait_ge(tanhs_done, g * (2 * NT) + (NT * u + t + 1))
                            if t % 2 == 0:
                                act.wait_ge(mixes_done, g * (2 * STEPS) + (STEPS * u + s + 1))
                            nc.scalar.activation(probs[:, s % 2, t % 2, kb * P:SEQ],
                                                 flat[:, 1024 * (t % 2) + kb * P:1024 * (t % 2) + SEQ],
                                                 ACT.Exp, scale=30.0).then_inc(exps_done, 1)

            @block.vector
            def _(dve):
                dve.wait_ge(key_aux_in, 16)
                for b in range(BATCH):
                    nc.vector.tensor_copy(keys_la[b][64:128, :], out_sb[64:128, :])
                nc.vector.memset(ones[:, :], 1.0).then_inc(setup, 1)
                nc.vector.memset(psum[:, 4:6, :], 0.0)
                nc.vector.memset(context_t[0][:, :], 0.0)
                nc.vector.memset(psum[:, DEN, :], 1.0).then_inc(setup, 1)
                dve.wait_ge(setup, 2)

                def split_weights(nth):
                    dve.wait_ge(w_loaded, nth * 16)
                    nc.vector.tensor_copy(wq_h[:, :, :], w_raw[:, :, 0:REP * HD1])
                    nc.vector.tensor_copy(wk_h[:, :, :, :], w_raw[:, :, REP * HD1:].unsqueeze(2)
                                          .broadcast_to([P, KC, 2, HD1])).then_inc(wh_done, 1)
                    dve.wait_ge(wh_done, nth)
                    nc.vector.tensor_tensor(wq_l[:, :, :], w_raw[:, :, 0:REP * HD1], wq_h[:, :, :], ALU.subtract)
                    nc.vector.tensor_tensor(wk_l[:, :, :, :], w_raw[:, :, REP * HD1:].unsqueeze(2)
                                            .broadcast_to([P, KC, 2, HD1]), wk_h[:, :, :, :],
                                            ALU.subtract).then_inc(w_split, 1)

                def rotate(r, slot, it, done):
                    if r is not None:
                        dve.wait_ge(split_done, r - 2)
                    nc.vector.tensor_tensor(straight[:, slot, :], psum[:, WORK, :],
                                            cos_sb[:, it[3] * 512:it[3] * 512 + 512], ALU.mult)
                    nc.vector.stream_shuffle(swapped[:, slot, :], psum[:, WORK, :], [i ^ 1 for i in range(32)])\
                        .then_inc(work_free, 1)

                def split(r, slot, it, unit_nth, first):
                    dve.wait_ge(roped, r)
                    h = it[3]
                    if it[0] == "q":
                        s = 2 * it[2] + h
                        if not (first and s < 2):
                            dve.wait_ge(placed[s % 2], unit_nth * 128 + 64 * (s // 2))
                        nc.vector.tensor_copy(high[:, s % 2, :], straight[:, slot, :]).then_inc(high_done, 1)
                        dve.wait_ge(high_done, r)
                        nc.vector.tensor_tensor(low[:, s % 2, :], straight[:, slot, :], high[:, s % 2, :],
                                                ALU.subtract).then_inc(split_done, 1)
                    else:
                        b, cols = it[1], slice(h * 512, h * 512 + 512)
                        nc.vector.tensor_copy(keys_hh[b][:, cols], straight[:, slot, :]).then_inc(high_done, 1)
                        dve.wait_ge(high_done, r)
                        nc.vector.tensor_tensor(keys_la[b][0:64, cols], straight[0:64, slot, :], keys_hh[b][0:64, cols],
                                                ALU.subtract).then_inc(split_done, 1)

                def take_out(mixes):
                    dve.wait_ge(mixes_done, mixes)
                    nc.vector.tensor_copy(out_sb[:, :], flat[:, OUT:OUT + SEQ])
                    nc.vector.tensor_copy(den_sb[:, :], psum[:, DEN, :]).then_inc(outs_free, 1)

                def finish(it):
                    bank = psum[:, WORK, :]
                    if it[0] == "den":
                        last = nc.vector.reciprocal(
                            recip[:, :, :].rearrange("p (j a) h -> p j a h", a=2),
                            bank.rearrange("p (j h a z) -> p j a h z", j=4, h=2, a=2)[:, :, :, :, 0])
                    elif it[0] == "ctx":
                        i = it[1]
                        last = nc.vector.tensor_tensor(
                            context[:, 4 * i:4 * i + 4, :].rearrange("p b (h d) -> p b h d", h=2),
                            bank.rearrange("p (b h d) -> p b h d", b=4, h=2),
                            recip[:, 4 * i:4 * i + 4, :].unsqueeze(3).broadcast_to([P, 4, 2, HD1]), ALU.mult)
                    elif it[0] == "back":
                        last = nc.vector.tensor_copy(context_t[it[2]][:, 512 * it[1]:512 * it[1] + 512], bank)
                    else:
                        t = NB * it[3] + 2 * it[1]
                        last = nc.vector.tensor_tensor(x[:, t:t + 2, :], bank.rearrange("p (t d) -> p t d", t=2),
                                                       x[:, t:t + 2, :], ALU.add)
                    last.then_inc(work_free, 1)

                split_weights(1)
                dve.wait_ge(tables, 32)
                for r, (n, it) in enumerate(FIRST):
                    dve.wait_ge(work_filled, n + 1)
                    rotate(r + 1 if r >= 2 else None, r % 2, it, n)
                    if r > 0:
                        split(r, (r - 1) % 2, FIRST[r - 1][1], 0, True)
                split(ROPES, (ROPES - 1) % 2, FIRST[-1][1], 0, True)
                with dve.Fori(0, G1, 1) as g:
                    for u in range(2):
                        rows = ropes(u)
                        for s in range(STEPS):
                            if s % NB == 0:
                                take_out(g * (2 * STEPS) + (STEPS * u + s + 2))
                            for n, it in PLANS[u][s]:
                                dve.wait_ge(work_filled, g * PER + (n + 1))
                                dve.wait_ge(work_free, g * PER + (n + 1))
                                if it[0] in "qk":
                                    r = rows[s][0][0]
                                    rotate(g * (2 * ROPES) + (ROPES * (u + 1) + r + 1), r % 2, it, n)
                                else:
                                    finish(it)
                            if s > 0:
                                for r, it in rows[s - 1]:
                                    split(g * (2 * ROPES) + (ROPES * (u + 1) + r + 1), r % 2, it,
                                          g * 2 + (u + 1), False)
                            if u == 0 and s == SPLIT_W:
                                split_weights(g + 2)
                take_out(2 * STEPS * G1 + 2)
                for n, it in LAST:
                    dve.wait_ge(work_filled, n + 1 + PER * (G1 - 1))
                    dve.wait_ge(work_free, n + 1 + PER * (G1 - 1))
                    finish(it)

            @block.tensor
            def _(pe):
                pe.sem_inc(work_free, 1)
                pe.sem_inc(mixes_done, 2)

                def item(done, it, weights, outs, turn):
                    bank = psum[:, WORK, :]
                    pe.wait_ge(work_free, done)
                    if it[0] in "qk":
                        pe.wait_ge(w_split, weights)
                        _, b, p, h = it
                        cols = slice(b * SEQ + h * 512, b * SEQ + h * 512 + 512)
                        if it[0] == "q":
                            w = [(wq_h[:, k, p * P:p * P + P], wq_l[:, k, p * P:p * P + P]) for k in range(KC)]
                        else:
                            w = [(wk_h[:, k, :, :].rearrange("p c d -> p (c d)"),
                                  wk_l[:, k, :, :].rearrange("p c d -> p (c d)")) for k in range(KC)]
                        last = three_pass(nc, bank, [(w[k], (xh[:, k, cols], xl[:, k, cols])) for k in range(KC)])
                    elif it[0] == "den":
                        pe.wait_ge(outs_free, outs)
                        for j in range(4):
                            last = nc.tensor.transpose(bank[:, j * P:j * P + P], den_sb[:, j * P:j * P + P], ident[:, :])
                    elif it[0] == "ctx":
                        for j in range(4):
                            at = (4 * it[1] + j) * P
                            last = nc.tensor.transpose(bank[:, j * P:j * P + P], out_sb[:, at:at + P], ident[:, :])
                    elif it[0] == "back":
                        for j in range(4):
                            last = nc.tensor.transpose(bank[:, j * P:j * P + P], context[:, 4 * it[1] + j, :], ident[:, :])
                    else:
                        if it[1] == 0:
                            pe.wait_ge(wo_loaded, turn * 16)
                        for j in range(2):
                            at = (2 * it[1] + j) * P
                            for p in range(2):
                                last = nc.tensor.matmul(bank[:, j * DM:j * DM + DM], context_t[p][:, at:at + P],
                                                        wo_sb[:, p, :], start=(p == 0), stop=(p == 1))
                    last.then_inc(work_filled, 1)

                def segments(kb):
                    return [(q0, q1) for q0, q1 in ((kb * P, 512), (max(kb * P, 512), SEQ)) if q0 < q1]

                def scores(g, u, t):
                    s, a = divmod(t, 2)
                    p, kb = divmod(s, NB)
                    pe.wait_ge(exps_done, g * (2 * NT) + (NT * u + t + 1))
                    at = slice(kb * P, kb * P + P)
                    for q0, q1 in segments(kb):
                        to = flat[:, 1024 * a + q0:1024 * a + q1]
                        nc.tensor.matmul(to, keys_hh[u][:, at], queries[u][:, 0, 2 * p + a, q0:q1], start=True,
                                         stop=False)
                        last = nc.tensor.matmul(to, keys_la[u][:, at], queries[u][:, 1, 2 * p + a, q0:q1], start=False,
                                                stop=True)
                    last.then_inc(scores_ready, 1)

                def mix(g, u, s):
                    p, kb = divmod(s, NB)
                    pe.wait_ge(masks_done, g * (2 * STEPS) + (STEPS * u + s + 1))
                    if kb == 0:
                        pe.wait_ge(outs_free, g * 4 + (2 * u + p + 1))
                    for q0, q1 in segments(kb):
                        for a in range(2):
                            nc.tensor.matmul(flat[64 * a:64 * a + 64, OUT + q0:OUT + q1], values[u][:, kb, :],
                                             probs[:, s % 2, a, q0:q1], start=(kb == 0),
                                             stop=(kb == (3 if q1 == 512 else NB - 1)))
                    for parity in range(2):
                        j = (kb - parity + 1) // 2
                        if j > 3:
                            continue
                        for a in range(2):
                            row = 32 * (2 * a + parity)
                            moving = probs[:, s % 2, a, :].rearrange("p (j c q) -> p j c q", j=4, c=2)[:, j:, parity, :]
                            last = nc.tensor.matmul(psum[row:row + 32, DEN, j * P:512], ones[:, :], moving,
                                                    start=(kb == 0), stop=(kb == 6 + parity))
                    last.then_inc(mixes_done, 1)

                pe.wait_ge(setup, 2)
                pe.wait_ge(zeros_set, 2)
                for n, it in FIRST:
                    item(n + 1, it, 1, 0, 0)
                with pe.Fori(0, G1, 1) as g:
                    for u in range(2):
                        for n in range(2):
                            pe.wait_ge(placed[n], g * 256 + 128 * (u + 1))
                        pe.wait_ge(split_done, g * (2 * ROPES) + ROPES * (u + 1))
                        pe.wait_ge(aux_loaded[u], g * 16 + 16)
                        pe.wait_ge(v_loaded[u], g * 16 + 16)
                        scores(g, u, 0)
                        scores(g, u, 1)
                        for s in range(STEPS):
                            if s + 1 < STEPS:
                                scores(g, u, 2 * s + 2)
                            for n, it in PLANS[u][s]:
                                item(g * PER + (n + 1), it, g + (u + 1), g * 4 + (2 * u + s // NB + 1),
                                     g + (u + 1))
                            if s + 1 < STEPS:
                                scores(g, u, 2 * s + 3)
                            mix(g, u, s)
                for n, it in LAST:
                    item(n + 1 + PER * (G1 - 1), it, 0, 4 * G1 + 1, G1 + 1)


def expert_ffn(nc, x, ident, psum, w1, b1, w2, b2, vt, u, select):
    with ExitStack() as ctx:
        sb = lambda n, s, d=FP32: ctx.enter_context(nc.sbuf_tensor(f"f1_{n}", s, d))
        sem = lambda n: ctx.enter_context(nc.semaphore(f"f1_{n}"))
        xh, xl = sb("xh", [P, KC, TOK], FP32R), sb("xl", [P, KC, TOK], FP32R)
        layer_norm(nc, "n3", x, xh, xl, ident, psum)
        w1_raw, v_raw = sb("w1_raw", [P, KC, DM]), sb("v_raw", [P, KC, ER * P])
        w1_h, w1_l = sb("w1_h", [P, KC, DM], FP32R), sb("w1_l", [P, KC, DM], FP32R)
        v_h, v_l = sb("v_h", [P, KC, ER * P], FP32R), sb("v_l", [P, KC, ER * P], FP32R)
        select_raw, select_sb = sb("select_raw", [P, ER, P]), sb("select", [P, ER, P], FP32R)
        w2_sb, u_sb = sb("w2", [P, KC, EXPERTS]), sb("u", [P, ER, DM])
        b1_sb, b2_sb = sb("b1", [P, KC]), sb("b2", [P, EXPERTS])
        hidden = sb("hidden", [P, KC, 512])
        vx = sb("vx", [P, ER, 512])
        logits, alphas = sb("logits", [P, 4, EXPERTS]), sb("alphas", [P, 4, EXPERTS])
        top, total = sb("top", [P, 4]), sb("total", [P, 4])
        alpha_h, alpha_l = sb("alpha_h", [P, 512], FP32R), sb("alpha_l", [P, 512], FP32R)
        mixed = sb("mixed", [P, ER, 512])
        loaded = [sem(f"loaded{n}") for n in range(4)]
        (v_seq, weights_ready, hidden_ready, hidden_done, vx_ready, vx_copied, logits_ready, shifted, exps_done,
         alphas_ready, turned, alpha_split, spread, mixed_done, out_ready, added) = map(sem, (
             "v_seq", "weights_ready", "hidden_ready", "hidden_done", "vx_ready", "vx_copied", "logits_ready",
             "shifted", "exps_done", "alphas_ready", "turned", "alpha_split", "spread", "mixed_done", "out_ready",
             "added"))
        BLOCKS = TOK // 512
        SETUP = 8
        PER = 5
        with nc.Block() as block:
            @block.sync
            def _(sp):
                for n, (to, of) in enumerate(((w1_raw, w1), (v_raw, vt), (select_raw, select))):
                    sp.dma_start(to[:, :, :], of).then_inc(loaded[n], 16)
                sp.dma_start(w2_sb[:, :, :], w2).then_inc(loaded[3], 16)
                sp.dma_start(u_sb[:, :, :], u).then_inc(loaded[3], 16)
                sp.dma_start(b1_sb[:, :], b1).then_inc(loaded[3], 16)
                sp.dma_start(b2_sb[:, :], b2.partition_broadcast(P)).then_inc(loaded[3], 16)

            @block.vector
            def _(dve):
                v = Chain(dve, v_seq)
                for n, (raw, h, l) in enumerate(((w1_raw, w1_h, w1_l), (v_raw, v_h, v_l))):
                    dve.wait_ge(loaded[n], 16)
                    v.link(nc.vector.tensor_copy(h[:, :, :], raw[:, :, :]))
                    v.link(nc.vector.tensor_tensor(l[:, :, :], raw[:, :, :], h[:, :, :], ALU.subtract))
                dve.wait_ge(loaded[2], 16)
                v.link(nc.vector.tensor_copy(select_sb[:, :, :], select_raw[:, :, :]))
                v.link(nc.vector.memset(alpha_h[:, :].bitcast(FP32), 0.0))
                v.link(nc.vector.memset(alpha_l[:, :].bitcast(FP32), 0.0))
                dve.wait_ge(loaded[3], 64)
                v.link(nc.vector.memset(total[:, :], 0.0))
                assert v.n == SETUP
                with dve.Fori(0, BLOCKS, 1) as i:
                    v = Chain(dve, v_seq, i * PER + SETUP)
                    for c in range(ER):
                        dve.wait_ge(vx_ready, i * ER + (c + 1))
                        nc.vector.tensor_copy(vx[:, c, :], psum[:, 2 + c, :]).then_inc(vx_copied, 1)
                    dve.wait_ge(logits_ready, i + 1)
                    v.link(nc.vector.tensor_tensor(logits[:, :, :],
                                                   psum[:, 6, 0:4 * EXPERTS].rearrange("p (t e) -> p t e", t=4),
                                                   b2_sb[:, :].unsqueeze(1).broadcast_to([P, 4, EXPERTS]), ALU.add))
                    v.link(nc.vector.reduce_max(top[:, :], logits[:, :, :], AXIS.X))
                    nc.vector.tensor_tensor(logits[:, :, :], logits[:, :, :],
                                            top[:, :].unsqueeze(2).broadcast_to([P, 4, EXPERTS]),
                                            ALU.subtract).then_inc(shifted, 1)
                    dve.wait_ge(exps_done, i + 1)
                    v.link(nc.vector.reduce_sum(total[:, :], alphas[:, :, :], AXIS.X))
                    v.link(nc.vector.reciprocal(total[:, :], total[:, :]))
                    nc.vector.tensor_tensor(alphas[:, :, :], alphas[:, :, :],
                                            total[:, :].unsqueeze(2).broadcast_to([P, 4, EXPERTS]),
                                            ALU.mult).then_inc(alphas_ready, 1)
                    dve.wait_ge(turned, i + 1)
                    v.link(nc.vector.tensor_copy(alpha_h[0:EXPERTS, :], psum[0:EXPERTS, 7, :]))
                    nc.vector.tensor_tensor(alpha_l[0:EXPERTS, :], psum[0:EXPERTS, 7, :], alpha_h[0:EXPERTS, :],
                                            ALU.subtract).then_inc(alpha_split, 1)
                    for c in range(ER):
                        dve.wait_ge(spread, i * ER + (c + 1))
                        nc.vector.tensor_tensor(mixed[:, c, :], psum[:, 6 * (c % 2), :], vx[:, c, :], ALU.mult)\
                            .then_inc(mixed_done, 1)
                    for t in range(4):
                        dve.wait_ge(out_ready, i * 4 + (t + 1))
                        rows = x[:, bass.ds(i * 4 + t, 1), :]
                        nc.vector.tensor_tensor(rows, psum[:, 2 + t:3 + t, 0:DM], rows, ALU.add).then_inc(added, 1)

            @block.scalar
            def _(act):
                act.wait_ge(v_seq, SETUP)
                with act.Fori(0, BLOCKS, 1) as i:
                    for m in range(KC):
                        act.wait_ge(hidden_ready, i * KC + (m + 1))
                        nc.scalar.activation(hidden[:, m, :], psum[:, m, :], ACT.Relu, bias=b1_sb[:, m:m + 1])\
                            .then_inc(hidden_done, 1)
                    act.wait_ge(shifted, i + 1)
                    nc.scalar.activation(alphas[:, :, :], logits[:, :, :], ACT.Exp).then_inc(exps_done, 1)

            @block.tensor
            def _(pe):
                pe.sem_inc(added, 4)
                pe.sem_inc(mixed_done, 2)
                pe.wait_ge(v_seq, SETUP)
                with pe.Fori(0, BLOCKS, 1) as i:
                    cols = bass.ds(i * 512, 512)
                    pe.wait_ge(mixed_done, i * ER + 2)
                    for m in range(KC):
                        at = slice(m * P, m * P + P)
                        three_pass(nc, psum[:, m, :], [((w1_h[:, k, at], w1_l[:, k, at]), (xh[:, k, cols], xl[:, k, cols]))
                                                       for k in range(KC)]).then_inc(hidden_ready, 1)
                    for c in range(ER):
                        at = slice(c * P, c * P + P)
                        pe.wait_ge(added, i * 4 + (c + 1))
                        three_pass(nc, psum[:, 2 + c, :], [((v_h[:, k, at], v_l[:, k, at]),
                                                            (xh[:, k, cols], xl[:, k, cols]))
                                                           for k in range(KC)]).then_inc(vx_ready, 1)
                    pe.wait_ge(hidden_done, i * KC + KC)
                    for t in range(4):
                        for k in range(KC):
                            last = nc.tensor.matmul(psum[:, 6, EXPERTS * t:EXPERTS * t + EXPERTS],
                                                    hidden[:, k, t * P:t * P + P], w2_sb[:, k, :],
                                                    start=(k == 0), stop=(k == KC - 1))
                    last.then_inc(logits_ready, 1)
                    pe.wait_ge(alphas_ready, i + 1)
                    for t in range(4):
                        last = nc.tensor.transpose(psum[0:EXPERTS, 7, t * P:t * P + P], alphas[:, t, :], ident[:, :])
                    last.then_inc(turned, 1)
                    pe.wait_ge(alpha_split, i + 1)
                    for c in range(ER):
                        pe.wait_ge(mixed_done, i * ER + (c + 1))
                        nc.tensor.matmul(psum[:, 6 * (c % 2), :], select_sb[:, c, :], alpha_h[:, :], start=True,
                                         stop=False)
                        nc.tensor.matmul(psum[:, 6 * (c % 2), :], select_sb[:, c, :], alpha_l[:, :], start=False,
                                         stop=True).then_inc(spread, 1)
                    pe.wait_ge(mixed_done, i * ER + (ER + 2))
                    for t in range(4):
                        pe.wait_ge(vx_copied, i * ER + ER)
                        for c in range(ER):
                            last = nc.tensor.matmul(psum[:, 2 + t, 0:DM], mixed[:, c, t * P:t * P + P], u_sb[:, c, :],
                                                    start=(c == 0), stop=(c == ER - 1))
                        last.then_inc(out_ready, 1)


def constants():
    import numpy as np

    def parts(v):
        out, rest = [], np.asarray(v, np.float64)
        for _ in range(3):
            bits = rest.astype(np.float32).view(np.uint32) & np.uint32(0xFFFFF000)
            out.append(bits.view(np.float32))
            rest = rest - out[-1].astype(np.float64)
        return out

    half = HD1 // 2
    inverse = (np.float32(1.0) / np.float32(10000.0) ** (np.arange(0, HD1, 2, dtype=np.float32) / np.float32(HD1)))
    angles = (np.arange(SEQ, dtype=np.float32)[:, None] * inverse.astype(np.float32)[None, :]).astype(np.float32)
    cosines = np.repeat(np.cos(angles.astype(np.float64)).astype(np.float32), 2, axis=1).T
    sines = np.repeat(np.sin(angles.astype(np.float64)).astype(np.float32), 2, axis=1).T
    sines = sines * np.where(np.arange(HD1) % 2 == 0, -1, 1).astype(np.float32)[:, None]
    slopes = (2.0 ** (-(np.arange(1, H1 + 1) * 8.0 / H1))).astype(np.float32).astype(np.float64)
    position = np.arange(SEQ, dtype=np.float64)
    aux = np.zeros((G1, AUX, REP, SEQ), np.float32)
    for h in range(H1):
        for n, part in enumerate(parts(slopes[h] * position) + parts(slopes[h] * np.ones(SEQ))):
            aux[h // REP, n, h % REP] = part
    key_aux = np.zeros((HD1, SEQ), np.float32)
    key_aux[0:3] = -1.0
    key_aux[3:6] = position
    select = np.zeros((P, ER, P), np.float32)
    for c in range(ER):
        for m in range(P):
            select[(c * P + m) // RANK, c, m] = 1.0
    return {"cosines": np.concatenate([cosines, cosines]), "sines": np.concatenate([sines, sines]),
            "aux": aux.reshape(G1 * AUX, REP * SEQ), "key_aux": key_aux, "select": select}


def build(nc, a, out):
    with ExitStack() as ctx:
        sb = lambda n, s, d=FP32: ctx.enter_context(nc.sbuf_tensor(n, s, d))
        sem = lambda n: ctx.enter_context(nc.semaphore(n))
        psum = ctx.enter_context(nc.psum_tensor("psum", [P, 8, 512], FP32))
        x = sb("rows", [P, TT, DM])
        ident = sb("ident", [P, P])
        ident_b = sb("ident_b", [P, P], BF16)
        mask_q = sb("mask_q", [P, P], BF16)
        mask_k = sb("mask_k", [P, P], BF16)
        keep = sb("keep", [P, P])
        loaded, made, stored = map(sem, ("loaded", "made", "stored"))
        with nc.Block() as block:
            @block.sync
            def _(sp):
                sp.dma_start(x[:, :, :], a["x"]).then_inc(loaded, 16)
                sp.wait_ge(loaded, 16)

            @block.gpsimd
            def _(pool):
                for n, t in enumerate((ident, ident_b, mask_q, mask_k, keep)):
                    nc.gpsimd.memset(t[:, :], 1.0 if n == 4 else 0.0).then_inc(made, 1)
                    pool.wait_ge(made, 2 * n + 1)
                    if n < 2:
                        nc.gpsimd.affine_select(out=t[:, :], in_=t[:, :], compare_op=ALU.not_equal, fill=1.0, base=0,
                                                pattern=[[-1, P]], channel_multiplier=1).then_inc(made, 1)
                    else:
                        sign = 1 if n == 2 else -1
                        nc.gpsimd.affine_select(out=t[:, :], in_=t[:, :], compare_op=ALU.is_ge, base=0,
                                                fill=-1e30 if n < 4 else 0.0,
                                                pattern=[[-sign, P]], channel_multiplier=sign).then_inc(made, 1)
                    pool.wait_ge(made, 2 * n + 2)

        layer0_attention(nc, x, ident, ident_b, mask_q, mask_k, psum, a["wq0"], a["wk0"], a["wv0"], a["wo0"])
        ternary_ffn(nc, x, ident, psum, a["w1"], a["w3"], a["w2"])
        layer1_attention(nc, x, ident, keep, psum, a["wqk1"], a["wv1"], a["wo1"], a["bo1"], a["aux"], a["key_aux"],
                         a["cosines"], a["sines"])
        expert_ffn(nc, x, ident, psum, a["e_w1"], a["e_b1"], a["e_w2"], a["e_b2"], a["e_vt"], a["e_u"], a["select"])
        with nc.Block() as block:
            @block.sync
            def _(sp):
                sp.dma_start(out, x[:, :, :]).then_inc(stored, 16)
                sp.wait_ge(stored, 16)


def kernel(**inputs):
    import numpy as np
    import concourse.bacc as bacc
    from concourse.bass_utils import run_bass_kernel_spmd

    def rows(w):
        w = np.ascontiguousarray(w)
        return np.ascontiguousarray(w.reshape(-1, P, w.shape[1]).transpose(1, 0, 2))

    i = {k: np.asarray(v) for k, v in inputs.items()}
    arrays = {
        "x": np.ascontiguousarray(i["L0_attn_x"].reshape(TT, P, DM).transpose(1, 0, 2)),
        "wq0": rows(i["L0_attn_wq"].T), "wk0": rows(i["L0_attn_wk"].T), "wv0": rows(i["L0_attn_wv"].T),
        "wo0": rows(i["L0_attn_wo"].T),
        "w1": rows(np.pad(i["L0_ffn_w1"], ((0, HC * P - HID), (0, 0))).T),
        "w3": rows(np.pad(i["L0_ffn_w3"], ((0, HC * P - HID), (0, 0))).T),
        "w2": rows(np.pad(i["L0_ffn_w2"], ((0, 0), (0, HC * P - HID))).T),
        "wqk1": np.ascontiguousarray(np.concatenate(
            [i["L1_attn_Wq"].reshape(KC, P, G1, REP * HD1), i["L1_attn_Wk"].reshape(KC, P, G1, HD1)], axis=3)
            .transpose(2, 1, 0, 3)).reshape(G1, P, KC * (REP + 1) * HD1),
        "wv1": rows(i["L1_attn_Wv"]),
        "wo1": np.ascontiguousarray(i["L1_attn_Wo"].reshape(G1, 2, P, DM).transpose(0, 2, 1, 3)).reshape(G1, P, 2 * DM),
        "bo1": i["L1_attn_bo"],
        "e_w1": rows(i["L1_ffn_W1"]), "e_w2": rows(i["L1_ffn_W2"]),
        "e_b1": np.ascontiguousarray(i["L1_ffn_b1"].reshape(KC, P).T), "e_b2": i["L1_ffn_b2"],
        "e_vt": rows(i["L1_ffn_V"].reshape(EXPERTS * RANK, DM).T),
        "e_u": rows(i["L1_ffn_U"].transpose(0, 2, 1).reshape(EXPERTS * RANK, DM)),
        **constants(),
    }
    nc = bacc.Bacc("TRN2", target_bir_lowering=False, num_devices=1)
    a = {n: nc.dram_tensor(n, list(v.shape), FP32, kind="ExternalInput").ap() for n, v in arrays.items()}
    out = nc.dram_tensor("out", [P, TT, DM], FP32, kind="ExternalOutput").ap()
    build(nc, a, out)
    got = run_bass_kernel_spmd(nc, [arrays], core_ids=[0]).results[0]["out"]
    return np.asarray(got).transpose(1, 0, 2).reshape(BATCH, SEQ, DM)
```

```python
import concourse.bass as bass
from concourse import mybir
from contextlib import ExitStack

FP32 = mybir.dt.float32
FP32R = mybir.dt.float32r
BF16 = mybir.dt.bfloat16
ALU = mybir.AluOpType
ACT = mybir.ActivationFunctionType
AXIS = mybir.AxisListType

P = 128
BATCH, SEQ, DM = 2, 1024, 256
TOK = BATCH * SEQ
TT = TOK // P
KC = DM // P
NB = SEQ // P
H0, HD0 = 16, 16
H1, G1, HD1 = 32, 8, 64
REP = H1 // G1
HID = int(2 * DM * 4 / 3)
HC = -(-HID // P)
HLAST = HID - (HC - 1) * P
EXPERTS, RANK = 8, 64
ER = EXPERTS * RANK // P
AUX = 6
EPS = 1e-5
LOWEST = -3e38


class Chain:

    def __init__(self, engine, semaphore, base=0):
        self.engine, self.semaphore, self.n, self.base = engine, semaphore, 0, base

    def link(self, instruction):
        self.n += 1
        instruction.then_inc(self.semaphore, 1)
        self.engine.wait_ge(self.semaphore, self.base + self.n)


def layer_norm(nc, name, x, xh, xl, ident, psum):
    with ExitStack() as ctx:
        sb = lambda n, s, d=FP32: ctx.enter_context(nc.sbuf_tensor(f"{name}_{n}", s, d))
        sem = lambda n: ctx.enter_context(nc.semaphore(f"{name}_{n}"))
        stats = sb("stats", [P, TT, 6])
        mean_var = sb("mean_var", [P, TT, 2])
        var_eps = sb("var_eps", [P, TT])
        std = sb("std", [P, TT])
        rstd = sb("rstd", [P, TT])
        xn = sb("xn", [P, 8, DM])
        v_seq, std_ready, rows_ready, turned, high_ready, low_ready = map(
            sem, ("v_seq", "std_ready", "rows_ready", "turned", "high_ready", "low_ready"))
        with nc.Block() as block:
            @block.vector
            def _(dve):
                for t in range(TT):
                    last = nc.vector.bn_stats(stats[:, t, :], x[:, t, :])
                last.then_inc(v_seq, 1)
                dve.wait_ge(v_seq, 1)
                for t in range(TT):
                    last = nc.vector.bn_aggr(mean_var[:, t, :], stats[:, t, :])
                last.then_inc(v_seq, 1)
                dve.wait_ge(v_seq, 2)
                nc.vector.tensor_scalar(var_eps[:, :], mean_var[:, :, 1], EPS, None, ALU.add).then_inc(v_seq, 1)
                dve.wait_ge(std_ready, 1)
                nc.vector.reciprocal(rstd[:, :], std[:, :]).then_inc(v_seq, 1)
                dve.wait_ge(v_seq, 4)
                for half in range(2):
                    for q in range(2):
                        for t in range(4):
                            tile = 8 * half + 4 * q + t
                            if half == 1 and t == 0:
                                dve.wait_ge(turned, q + 1)
                            last = nc.vector.tensor_scalar(xn[:, 4 * q + t, :], x[:, tile, :], mean_var[:, tile, 0:1],
                                                           rstd[:, tile:tile + 1], ALU.subtract, ALU.mult)
                        last.then_inc(rows_ready, 1)
                    for q in range(2):
                        group = 2 * half + q
                        dve.wait_ge(high_ready, group + 1)
                        for c in range(KC):
                            cols = slice(group * 512, group * 512 + 512)
                            last = nc.vector.tensor_tensor(xl[:, c, cols], psum[:, 2 * q + c, :], xh[:, c, cols],
                                                           ALU.subtract)
                        last.then_inc(low_ready, 1)

            @block.scalar
            def _(act):
                act.wait_ge(v_seq, 3)
                nc.scalar.activation(std[:, :], var_eps[:, :], ACT.Sqrt).then_inc(std_ready, 1)
                for group in range(4):
                    act.wait_ge(turned, group + 1)
                    for c in range(KC):
                        cols = slice(group * 512, group * 512 + 512)
                        last = nc.scalar.activation(xh[:, c, cols], psum[:, 2 * (group % 2) + c, :], ACT.Copy)
                    last.then_inc(high_ready, 1)

            @block.tensor
            def _(pe):
                for group in range(4):
                    pe.wait_ge(rows_ready, group + 1)
                    if group >= 2:
                        pe.wait_ge(low_ready, group - 1)
                    for t in range(4):
                        for c in range(KC):
                            last = nc.tensor.transpose(psum[:, 2 * (group % 2) + c, t * P:(t + 1) * P],
                                                       xn[:, 4 * (group % 2) + t, c * P:(c + 1) * P], ident[:, :])
                    last.then_inc(turned, 1)


def three_pass(nc, out, pairs):
    terms = []
    for (ah, al), (bh, bl) in pairs:
        terms += [(ah, bh), (al, bh), (ah, bl)]
    for n, (a, b) in enumerate(terms):
        last = nc.tensor.matmul(out, a, b, start=(n == 0), stop=(n == len(terms) - 1))
    return last


def layer0_attention(nc, x, ident, ident_b, mask_q, mask_k, psum, wq0, wk0, wv0, wo0):
    with ExitStack() as outer:
        osb = lambda n, s, d=FP32: outer.enter_context(nc.sbuf_tensor(f"a0_{n}", s, d))
        qh, ql = osb("qh", [P, 4, SEQ]), osb("ql", [P, 4, SEQ])
        kh, kl = osb("kh", [P, 4, SEQ]), osb("kl", [P, 4, SEQ])
        v0 = osb("v0", [P, TT, DM])
        scratch = [nc.dram_tensor(f"{n}_scratch", [2, 4, P, SEQ], FP32).ap() for n in ("query", "key")]
        stored = outer.enter_context(nc.semaphore("a0_stored"))

        with ExitStack() as ctx:
            sb = lambda n, s, d=FP32: ctx.enter_context(nc.sbuf_tensor(f"p0_{n}", s, d))
            sem = lambda n: ctx.enter_context(nc.semaphore(f"p0_{n}"))
            xh, xl = sb("xh", [P, KC, TOK], FP32R), sb("xl", [P, KC, TOK], FP32R)
            layer_norm(nc, "n0", x, xh, xl, ident, psum)
            raw = [sb(f"raw{n}", [P, KC, DM]) for n in range(3)]
            wh = [sb(f"wh{n}", [P, KC, DM], FP32R) for n in range(3)]
            wl = [sb(f"wl{n}", [P, KC, DM], FP32R) for n in range(3)]
            loaded = [sem(f"loaded{n}") for n in range(3)]
            split, product, high_ready, bank_free, v_seq = map(
                sem, ("split", "product", "high_ready", "bank_free", "v_seq"))
            dst = {0: (qh, ql), 1: (kh, kl)}
            items = [(w, c, tb) for w in range(2) for c in range(KC) for tb in range(4)]
            items += [(2, None, t) for t in range(TT)]
            BANKS = 8

            with nc.Block() as block:
                @block.sync
                def _(sp):
                    for n, w in enumerate((wq0, wk0, wv0)):
                        sp.dma_start(raw[n][:, :, :], w).then_inc(loaded[n], 16)
                    for n, (w, c, t) in enumerate(items):
                        if w < 2 and t % 2 == 1:
                            sp.wait_ge(bank_free, n + 1)
                            slot = 2 * (t // 2) + c
                            for part, tile in enumerate(dst[w]):
                                sp.dma_start(scratch[w][part, slot, :, :], tile[:, slot, :]).then_inc(stored, 16)

                @block.tensor
                def _(pe):
                    for n, (w, c, t) in enumerate(items):
                        if n == 0 or items[n - 1][0] != w:
                            pe.wait_ge(split, w + 1)
                        if n >= BANKS:
                            pe.wait_ge(bank_free, n - BANKS + 1)
                        if w < 2:
                            m = slice(c * P, (c + 1) * P)
                            cols = slice(t * 512, t * 512 + 512)
                            three_pass(nc, psum[:, n % BANKS, :],
                                       [((wh[w][:, k, m], wl[w][:, k, m]), (xh[:, k, cols], xl[:, k, cols]))
                                        for k in range(KC)]).then_inc(product, 1)
                        else:
                            cols = slice(t * P, (t + 1) * P)
                            three_pass(nc, psum[:, n % BANKS, 0:DM],
                                       [((xh[:, k, cols], xl[:, k, cols]), (wh[2][:, k, :], wl[2][:, k, :]))
                                        for k in range(KC)]).then_inc(product, 1)

                @block.scalar
                def _(act):
                    for n, (w, c, t) in enumerate(items):
                        if w == 2:
                            continue
                        high = dst[w][0]
                        part = high[:, 2 * (t // 2) + c, 512 * (t % 2):512 * (t % 2) + 512]
                        act.wait_ge(product, n + 1)
                        nc.scalar.activation(part.bitcast(FP32R), psum[:, n % BANKS, :], ACT.Copy)\
                            .then_inc(high_ready, 1)

                @block.vector
                def _(dve):
                    for w in range(3):
                        dve.wait_ge(loaded[w], 16)
                        nc.vector.tensor_copy(wh[w][:, :, :], raw[w][:, :, :]).then_inc(v_seq, 1)
                        dve.wait_ge(v_seq, w + 1)
                        nc.vector.tensor_tensor(wl[w][:, :, :], raw[w][:, :, :], wh[w][:, :, :],
                                                ALU.subtract).then_inc(split, 1)
                    for n, (w, c, t) in enumerate(items):
                        if w == 2:
                            dve.wait_ge(product, n + 1)
                            nc.vector.tensor_copy(v0[:, t, :], psum[:, n % BANKS, 0:DM]).then_inc(bank_free, 1)
                            continue
                        high, low = dst[w]
                        at = (slice(None), 2 * (t // 2) + c, slice(512 * (t % 2), 512 * (t % 2) + 512))
                        dve.wait_ge(high_ready, n + 1)
                        nc.vector.tensor_tensor(low[at].bitcast(FP32R), psum[:, n % BANKS, :], high[at],
                                                ALU.subtract).then_inc(bank_free, 1)


        QUAD = 4
        TURNS = BATCH * H0 // (2 * QUAD)
        with ExitStack() as ctx:
            sb = lambda n, s, d=FP32: ctx.enter_context(nc.sbuf_tensor(f"s0_{n}", s, d))
            sem = lambda n: ctx.enter_context(nc.semaphore(f"s0_{n}"))
            q3 = [sb(f"q3_{n}", [P, QUAD, SEQ], FP32R) for n in range(2)]
            k3 = [sb(f"k3_{n}", [P, QUAD, SEQ], FP32R) for n in range(2)]
            probs = sb("probs", [P, 2, QUAD, SEQ])
            values = [sb(f"values{n}", [P, NB, QUAD, 32]) for n in range(2)]
            part_max = sb("part_max", [P, QUAD, NB, 2])
            neg_max = sb("neg_max", [P, QUAD * NB])
            max_high, max_low = sb("max_high", [QUAD * NB, P], FP32R), sb("max_low", [QUAD * NB, P], FP32R)
            out_sb = sb("out_sb", [P, SEQ])
            recip = sb("recip", [P, 4, QUAD])
            loaded = [[sem(f"loaded{q}{h}") for h in range(2)] for q in range(2)]
            (max_rows, values_ready, small_filled, small_free, scores_ready, exps_done, pvs_done, outs_copied,
             neg_ready, high_done, recip_done, setup, ones_set, any_set) = map(sem, (
                 "max_rows", "values_ready", "small_filled", "small_free", "scores_ready", "exps_done",
                 "pvs_done", "outs_copied", "neg_ready", "high_done", "recip_done", "setup",
                 "ones_set", "any_set"))
            flat = psum[:, :, :].rearrange("p a b -> p (a b)")
            RING = 3
            OUT = 3 * 512
            small_bank = lambda n: 5 + n % RING
            qh_flat = qh[:, :, :].rearrange("p t d -> p (t d)")
            v0_flat = v0[:, :, :].rearrange("p t d -> p (t d)")

            SEGS = [(qb, h, s, min(512, P * (qb + 1) - 512 * s))
                    for qb in range(NB) for h in range(QUAD) for s in range(1 + qb // 4)]
            GROUPS = [(kb, max(kb * P, 512 * half), 512 * half + 512) for kb in range(NB) for half in range(2)
                      if kb * P < 512 * half + 512]
            STEPS = [(kb, h, q0, q1) for kb, q0, q1 in GROUPS for h in range(QUAD)]
            NEAR = sum(QUAD for kb, _, _ in GROUPS if kb < 4)

            NT = len(STEPS)
            LOAD = 16 * 7
            MAX_STEPS, TURN_STEP = 34, 37
            OUT_STEPS = (8, 11)

            def plan(n):
                own = [sum(q1 - q0 + P for _, _, q0, q1 in STEPS[:t + 1]) for t in range(MAX_STEPS)]
                cost = [64 + width for _, _, _, width in SEGS]
                steps, seg = [[] for _ in STEPS], 0
                for t in range(MAX_STEPS):
                    while seg < len(SEGS) and sum(cost[:seg]) * own[-1] < own[t] * sum(cost):
                        steps[t].append(("max", seg))
                        seg += 1
                steps[TURN_STEP].append(("turn", 0))
                for arg, t in enumerate(OUT_STEPS):
                    steps[t].append(("out", arg))
                numbered = []
                for step in steps:
                    numbered.append([(n + i, kind, arg) for i, (kind, arg) in enumerate(step)])
                    n += len(step)
                return numbered, n

            AHEAD = len(SEGS) + 1
            plan_a, n_b = plan(AHEAD)
            plan_b, n_tail = plan(n_b)
            PLANS = [plan_a, plan_b]
            PER = n_tail - AHEAD
            TAIL = [(n_tail, "out", 0), (n_tail + 1, "out", 1)]
            assert PER % RING == 0 and NT % RING == 0
            FIRST = [(n, "max", n) for n in range(len(SEGS))] + [(len(SEGS), "turn", 0)]
            FAR_SEG = min(n for n, seg in enumerate(SEGS) if seg[0] == 4)
            OUT_ITEM, TURN_ITEM = ([n for p in PLANS for step in p for n, kind, arg in step if (kind, arg) == item]
                                   for item in (("out", 1), ("turn", 0)))

            with nc.Block() as block:
                @block.sync
                def _(sp):
                    def load(quad, half, slot):
                        cols = slice(512 * half, 512 * half + 512)
                        for w, (to, order) in enumerate(((q3[quad], (0, 1, 0)), (k3[quad], (0, 0, 1)))):
                            for row, part in enumerate(order):
                                src = scratch[w][part, bass.ds(slot, 1), 64 * quad:64 * quad + 64, cols]
                                sp.dma_start(to[16 * row:16 * row + 16, :, cols].bitcast(FP32),
                                             src.rearrange("o (h d) n -> d (o h) n", h=QUAD))\
                                    .then_inc(loaded[quad][half], 16)
                        sp.dma_start(q3[quad][48:50, :, cols].bitcast(FP32), q3[quad][100:102, :, cols].bitcast(FP32))\
                            .then_inc(loaded[quad][half], 16)

                    def put_max(quad, turn_item):
                        sp.wait_ge(small_free, turn_item + (RING + 1))
                        for row, part in ((48, max_high), (49, max_low)):
                            sp.dma_start(q3[quad][row:row + 1, :, :].rearrange("o h n -> o (h n)").bitcast(FP32),
                                         part[:, :].bitcast(FP32)).then_inc(max_rows, 16)

                    sp.wait_ge(setup, 7)
                    sp.wait_ge(stored, 16 * 16)
                    for quad in range(2):
                        for half in range(2):
                            load(quad, half, 0)
                    put_max(0, AHEAD - 1)
                    with sp.Fori(0, TURNS, 1) as j:
                        for quad in range(2):
                            sp.wait_ge(scores_ready, j * (2 * NT) + NT * quad + NEAR)
                            load(quad, 0, (j + 1) % TURNS)
                            put_max(1 - quad, j * PER + TURN_ITEM[quad])
                            sp.wait_ge(scores_ready, j * (2 * NT) + NT * quad + NT)
                            load(quad, 1, (j + 1) % TURNS)
                    for quad in range(2):
                        for half in range(2):
                            sp.wait_ge(loaded[quad][half], LOAD * (TURNS + 1))
                    sp.wait_ge(max_rows, 32 * (2 * TURNS + 1))

                @block.gpsimd
                def _(pool):
                    def gather(quad, slot):
                        for kb in range(NB):
                            src = v0_flat[:, bass.ds((slot // 2) * (NB * DM) + (slot % 2) * P + kb * DM + 64 * quad, 64)]
                            last = nc.gpsimd.tensor_copy(values[quad][:, kb, :, 0:HD0],
                                                         src.rearrange("p (h d) -> p h d", h=QUAD))
                        last.then_inc(values_ready, 1)

                    for n in range(2):
                        nc.gpsimd.memset(q3[n][:, :, :].bitcast(FP32), 0.0).then_inc(setup, 1)
                        nc.gpsimd.memset(k3[n][:, :, :].bitcast(FP32), 1.0).then_inc(setup, 1)
                    pool.wait_ge(ones_set, 2)
                    gather(0, 0)
                    gather(1, 0)
                    with pool.Fori(0, TURNS, 1) as j:
                        for quad in range(2):
                            pool.wait_ge(pvs_done, j * (2 * NB) + NB * quad + NB + 2)
                            gather(quad, (j + 1) % TURNS)

                @block.vector
                def _(dve):
                    nc.vector.memset(part_max[:, :, :, :], LOWEST).then_inc(setup, 1)
                    for n in range(2):
                        nc.vector.memset(values[n][:, :, :, :], 0.0).then_inc(setup, 1)
                    dve.wait_ge(setup, 7)
                    for n in range(2):
                        nc.vector.memset(values[n][:, :, :, HD0:HD0 + 1], 1.0).then_inc(ones_set, 1)
                    nc.vector.memset(probs[:, 1, :, :], 1.0)
                    nc.vector.memset(flat[:, OUT:OUT + 512], 1.0).then_inc(any_set, 1)
                    for quad in range(2):
                        for half in range(2):
                            dve.wait_ge(loaded[quad][half], LOAD)

                    def small(j, n, kind, arg, quad, nth, slot=None):
                        done = n if j is None else j * PER + n
                        bank = psum[:, small_bank(n), :]
                        if kind != "max":
                            dve.wait_ge(small_free, done + RING)
                        if kind == "turn":
                            nc.vector.tensor_reduce(
                                neg_max[:, :], part_max[:, :, :, :].rearrange("p h b s -> p (h b) s"),
                                axis=AXIS.X, op=ALU.max, negate=True).then_inc(neg_ready, 1)
                        dve.wait_ge(small_filled, done + 1)
                        if kind == "max":
                            qb, h, s, width = SEGS[arg]
                            nc.vector.reduce_max(part_max[:, h, qb, s:s + 1], bank[:, 0:width], AXIS.X)\
                                .then_inc(small_free, 1)
                        elif kind == "turn":
                            if j is not None:
                                dve.wait_ge(max_rows, nth * 32)
                            nc.vector.tensor_copy(max_high[:, :], bank[0:QUAD * NB, 0:P]).then_inc(high_done, 1)
                            dve.wait_ge(high_done, nth + 1)
                            nc.vector.tensor_tensor(max_low[:, :], bank[0:QUAD * NB, 0:P], max_high[:, :],
                                                    ALU.subtract).then_inc(small_free, 1)
                        else:
                            view = bank.rearrange("p (b h d) -> p b h d", b=4, h=QUAD)
                            nc.vector.reciprocal(recip[:, :, :], view[:, :, :, HD0]).then_inc(recip_done, 1)
                            dve.wait_ge(recip_done, nth + 1)
                            to = qh_flat[:, bass.ds(slot * SEQ + 512 * arg, 512)].rearrange("p (b c) -> p b c", b=4)
                            nc.vector.tensor_tensor(
                                to[:, :, 64 * quad:64 * quad + 64].rearrange("p b (h d) -> p b h d", h=QUAD),
                                view[:, :, :, 0:HD0], recip[:, :, :].unsqueeze(3).broadcast_to([P, 4, QUAD, HD0]),
                                ALU.mult).then_inc(small_free, 1)

                    for n, kind, arg in FIRST:
                        small(None, n, kind, arg, 0, 0)
                    with dve.Fori(0, TURNS, 1) as j:
                        for quad in range(2):
                            for step in PLANS[quad]:
                                for n, kind, arg in step:
                                    if kind == "out":
                                        slot = j if quad == 1 else j * (TURNS - 1) // TURNS
                                        small(j, n, kind, arg, 1 - quad, j * 4 + (2 * quad + arg), slot)
                                    else:
                                        small(j, n, kind, arg, 1 - quad, j * 2 + (quad + 1))
                    for n, kind, arg in TAIL:
                        small(TURNS - 1, n, kind, arg, 1, TURNS * 4 + arg, TURNS - 1)

                @block.scalar
                def _(act):
                    act.sem_inc(exps_done, RING)

                    def take_out(pvs, read):
                        act.wait_ge(pvs_done, pvs)
                        act.wait_ge(small_filled, read)
                        nc.scalar.activation(out_sb[:, :], flat[:, OUT:OUT + SEQ], ACT.Copy)\
                            .then_inc(outs_copied, 1)

                    with act.Fori(0, TURNS, 1) as j:
                        for quad in range(2):
                            for t, (kb, h, q0, q1) in enumerate(STEPS):
                                act.wait_ge(scores_ready, j * (2 * NT) + (NT * quad + t + 1))
                                if h == 0 and q0 == kb * P:
                                    act.wait_ge(pvs_done, j * (2 * NB) + (NB * quad + kb + 1))
                                nc.scalar.activation(probs[:, kb % 2, h, q0:q1],
                                                     psum[:, t % RING, q0 % 512:q0 % 512 + q1 - q0],
                                                     ACT.Exp, scale=HD0 ** -0.5).then_inc(exps_done, 1)
                                if t == 3:
                                    take_out(j * (2 * NB) + (NB * quad + 2),
                                             j * PER + (OUT_ITEM[0] + 1 if quad else OUT_ITEM[1] + 1 - PER))
                    take_out(TURNS * 2 * NB + 2, (TURNS - 1) * PER + OUT_ITEM[1] + 1)

                @block.tensor
                def _(pe):
                    pe.sem_inc(small_free, RING)
                    pe.sem_inc(pvs_done, 1)

                    def small(j, n, kind, arg, quad, nth):
                        done = n if j is None else j * PER + n
                        bank = psum[:, small_bank(n), :]
                        pe.wait_ge(small_free, done + 1)
                        if kind == "max":
                            qb, h, s, width = SEGS[arg]
                            if arg in (0, FAR_SEG):
                                half = int(arg > 0)
                                pe.wait_ge(loaded[quad][half], nth * LOAD)
                            diagonal = s == qb // 4
                            last = nc.tensor.matmul(bank[:, 0:width], q3[quad][:, h, qb * P:qb * P + P],
                                                    k3[quad][:, h, 512 * s:512 * s + width], start=True,
                                                    stop=not diagonal)
                            if diagonal:
                                last = nc.tensor.matmul(bank[:, width - P:width], ident_b[:, :], mask_q[:, :],
                                                        start=False, stop=True)
                        elif kind == "turn":
                            pe.wait_ge(neg_ready, nth)
                            last = nc.tensor.transpose(bank[0:QUAD * NB, 0:P], neg_max[:, :], ident[:, :])
                        else:
                            pe.wait_ge(outs_copied, nth)
                            for b in range(4):
                                at = (4 * arg + b) * P
                                last = nc.tensor.transpose(bank[:, b * P:b * P + P], out_sb[:, at:at + P], ident[:, :])
                        last.then_inc(small_filled, 1)

                    def scores(j, quad, t):
                        kb, h, q0, q1 = STEPS[t]
                        pe.wait_ge(exps_done, j * (2 * NT) + (NT * quad + t + 1))
                        to = psum[:, t % RING, q0 % 512:q0 % 512 + q1 - q0]
                        diagonal = q0 == kb * P
                        last = nc.tensor.matmul(to, k3[quad][:, h, kb * P:kb * P + P], q3[quad][:, h, q0:q1],
                                                start=True, stop=not diagonal)
                        if diagonal:
                            last = nc.tensor.matmul(to[:, 0:P], ident_b[:, :], mask_k[:, :], start=False, stop=True)
                        last.then_inc(scores_ready, 1)

                    def mix(j, quad, n):
                        v = quad if n >= 0 else 1 - quad
                        kb, q0, q1 = GROUPS[n]
                        pe.wait_ge(exps_done, j * (2 * NT) + (NT * quad + QUAD * (n + 1) + RING))
                        if n == 0:
                            pe.wait_ge(outs_copied, j * 2 + (quad + 1))
                            pe.wait_ge(values_ready, j * 2 + (quad + 1))
                        for h in range(QUAD):
                            last = nc.tensor.matmul(flat[32 * h:32 * h + 32, OUT + q0:OUT + q1], values[v][:, kb, h, :],
                                                    probs[:, kb % 2, h, q0:q1], start=(kb == 0),
                                                    stop=(kb == (3 if q1 == 512 else NB - 1)))
                        if q1 == SEQ:
                            last.then_inc(pvs_done, 1)

                    for n, kind, arg in FIRST:
                        small(None, n, kind, arg, 0, 1)
                    pe.wait_ge(any_set, 1)
                    pe.wait_ge(values_ready, 2)
                    for h in range(QUAD):
                        nc.tensor.matmul(flat[32 * h:32 * h + 32, OUT + 512:OUT + SEQ], values[1][:, 0, h, :],
                                         probs[:, 1, h, 0:512], start=True, stop=False)
                    with pe.Fori(0, TURNS, 1) as j:
                        for quad in range(2):
                            for t in range(NT):
                                if t == 0:
                                    pe.wait_ge(max_rows, j * 64 + 32 * (quad + 1))
                                scores(j, quad, t)
                                if t % QUAD == 2:
                                    mix(j, quad, t // QUAD - 1)
                                for n, kind, arg in PLANS[quad][t]:
                                    nth = {"max": j + (quad + 1), "turn": j * 2 + (quad + 2),
                                           "out": j * 2 + (quad + 1)}[kind]
                                    small(j, n, kind, arg, 1 - quad, nth)
                    mix(TURNS, 0, -1)
                    for n, kind, arg in TAIL:
                        small(TURNS - 1, n, kind, arg, 1, TURNS * 2 + 1)

        with ExitStack() as ctx:
            sb = lambda n, s, d=FP32: ctx.enter_context(nc.sbuf_tensor(f"o0_{n}", s, d))
            sem = lambda n: ctx.enter_context(nc.semaphore(f"o0_{n}"))
            weights = sb("weights", [P, KC, DM])
            turned_sb = sb("turned", [P, 2, KC * P])
            loaded, turned, copied, product, added = map(sem, ("loaded", "turned", "copied", "product", "added"))
            with nc.Block() as block:
                @block.sync
                def _(sp):
                    sp.dma_start(weights[:, :, :], wo0).then_inc(loaded, 16)

                @block.tensor
                def _(pe):
                    pe.wait_ge(loaded, 16)

                    def turn(t):
                        if t >= 2:
                            pe.wait_ge(copied, t - 1)
                        b, qb = divmod(t, NB)
                        for c in range(KC):
                            last = nc.tensor.transpose(psum[:, t % 2, c * P:c * P + P],
                                                       qh[:, 2 * b + c, qb * P:qb * P + P], ident[:, :])
                        last.then_inc(turned, 1)

                    turn(0)
                    for t in range(TT):
                        if t + 1 < TT:
                            turn(t + 1)
                        pe.wait_ge(copied, t + 1)
                        if t >= 2:
                            pe.wait_ge(added, t - 1)
                        for c in range(KC):
                            last = nc.tensor.matmul(psum[:, 2 + t % 2, 0:DM], turned_sb[:, t % 2, c * P:c * P + P],
                                                    weights[:, c, :], start=(c == 0), stop=(c == KC - 1))
                        last.then_inc(product, 1)

                @block.scalar
                def _(act):
                    for t in range(TT):
                        act.wait_ge(turned, t + 1)
                        if t >= 2:
                            act.wait_ge(product, t - 1)
                        nc.scalar.activation(turned_sb[:, t % 2, :], psum[:, t % 2, 0:KC * P], ACT.Copy)\
                            .then_inc(copied, 1)

                @block.vector
                def _(dve):
                    for t in range(TT):
                        dve.wait_ge(product, t + 1)
                        nc.vector.tensor_tensor(x[:, t, :], psum[:, 2 + t % 2, 0:DM], x[:, t, :], ALU.add)\
                            .then_inc(added, 1)


def ternary_ffn(nc, x, ident, psum, w1, w3, w2):
    with ExitStack() as ctx:
        sb = lambda n, s, d=FP32: ctx.enter_context(nc.sbuf_tensor(f"f0_{n}", s, d))
        sem = lambda n: ctx.enter_context(nc.semaphore(f"f0_{n}"))
        xh, xl = sb("xh", [P, KC, TOK], FP32R), sb("xl", [P, KC, TOK], FP32R)
        layer_norm(nc, "n1", x, xh, xl, ident, psum)
        raw = [sb("raw1", [P, KC, HC * P]), sb("raw3", [P, KC, HC * P]), sb("raw2", [P, HC, DM])]
        below = sb("below", [P, HC * DM])
        signs = [sb("signs1", [P, KC, HC * P], FP32R), sb("signs3", [P, KC, HC * P], FP32R), sb("signs2", [P, HC, DM])]
        sums = sb("sums", [P, 3])
        scales = sb("scales", [P, 3])
        half, minus_half = sb("half", [P, 3]), sb("minus_half", [P, 3])
        scale_out = sb("scale_out", [P, 1])
        ones = sb("ones", [P, P])
        gate = sb("gate", [P, 2, 512])
        hidden = sb("hidden", [P, HC, 512])
        loaded = [sem(f"loaded{n}") for n in range(3)]
        (v_seq, summed, totals, signs_ready, up_ready, gates_done, hidden_done, out_ready, added) = map(sem, (
            "v_seq", "summed", "totals", "signs_ready", "up_ready", "gates_done", "hidden_done", "out_ready",
            "added"))
        BLOCKS = TOK // 512
        UP, OUT = (0, 2), 4

        with nc.Block() as block:
            @block.sync
            def _(sp):
                for n, w in enumerate((w1, w3, w2)):
                    sp.dma_start(raw[n][:, :, :], w).then_inc(loaded[n], 16)

            @block.vector
            def _(dve):
                v = Chain(dve, v_seq)
                v.link(nc.vector.memset(ones[:, :], 1.0))
                for n in range(3):
                    dve.wait_ge(loaded[n], 16)
                    last = nc.vector.tensor_reduce(sums[:, n:n + 1], raw[n][:, :, :], axis=AXIS.XY, op=ALU.add,
                                                   apply_absolute_value=True)
                last.then_inc(summed, 1)
                dve.wait_ge(totals, 1)
                v.link(nc.vector.tensor_scalar(scales[:, :], psum[:, 7, 0:3], 1.0 / (HID * DM), None, ALU.mult))
                v.link(nc.vector.tensor_scalar(half[:, :], scales[:, :], 0.5, None, ALU.mult))
                v.link(nc.vector.tensor_scalar(minus_half[:, :], scales[:, :], -0.5, None, ALU.mult))
                v.link(nc.vector.tensor_tensor(scale_out[:, :], scales[:, 1:2], scales[:, 2:3], ALU.mult))
                for n in range(3):
                    flat_raw = raw[n][:, :, :].rearrange("p a b -> p (a b)")
                    flat_signs = signs[n][:, :, :].rearrange("p a b -> p (a b)")
                    v.link(nc.vector.tensor_scalar(below[:, :], flat_raw, minus_half[:, n:n + 1], None, ALU.is_lt))
                    nc.vector.scalar_tensor_tensor(flat_signs, flat_raw, half[:, n:n + 1], below[:, :], ALU.is_gt,
                                                   ALU.subtract).then_inc(signs_ready, 1)
                    dve.wait_ge(signs_ready, n + 1)
                with dve.Fori(0, BLOCKS, 1) as i:
                    for c in range(HC):
                        dve.wait_ge(gates_done, i * HC + (c + 1))
                        nc.vector.tensor_tensor(hidden[:, c, :], psum[:, UP[1] + c % 2, :], gate[:, c % 2, :],
                                                ALU.mult).then_inc(hidden_done, 1)
                    for t in range(4):
                        dve.wait_ge(out_ready, i * 4 + (t + 1))
                        rows = x[:, bass.ds(i * 4 + t, 1), :]
                        nc.vector.scalar_tensor_tensor(rows, psum[:, OUT + t:OUT + t + 1, 0:DM], scale_out[:, :], rows,
                                                       ALU.mult, ALU.add).then_inc(added, 1)

            @block.scalar
            def _(act):
                act.wait_ge(signs_ready, 1)
                with act.Fori(0, BLOCKS, 1) as i:
                    for c in range(HC):
                        act.wait_ge(up_ready, i * HC + (c + 1))
                        act.wait_ge(hidden_done, i * HC + (c + 1))
                        nc.scalar.activation(gate[:, c % 2, :], psum[:, UP[0] + c % 2, :], ACT.Silu,
                                             scale=scales[:, 0:1]).then_inc(gates_done, 1)

            @block.tensor
            def _(pe):
                pe.sem_inc(hidden_done, 2)
                pe.sem_inc(added, 4)
                pe.wait_ge(summed, 1)
                nc.tensor.matmul(psum[:, 7, 0:3], ones[:, :], sums[:, :], start=True, stop=True).then_inc(totals, 1)
                pe.wait_ge(signs_ready, 3)
                with pe.Fori(0, BLOCKS, 1) as i:
                    for c in range(HC):
                        pe.wait_ge(hidden_done, i * HC + (c + 1))
                        for w in range(2):
                            n = 0
                            for k in range(KC):
                                for part in (xh, xl):
                                    last = nc.tensor.matmul(psum[:, UP[w] + c % 2, :],
                                                            signs[w][:, k, c * P:c * P + P],
                                                            part[:, k, bass.ds(i * 512, 512)],
                                                            start=(n == 0), stop=(n == 2 * KC - 1))
                                    n += 1
                        last.then_inc(up_ready, 1)
                    pe.wait_ge(hidden_done, i * HC + (HC + 2))
                    for t in range(4):
                        pe.wait_ge(added, i * 4 + (t + 1))
                        for c in range(HC):
                            last = nc.tensor.matmul(psum[:, OUT + t, 0:DM], hidden[:, c, t * P:t * P + P],
                                                    signs[2][:, c, :], start=(c == 0), stop=(c == HC - 1))
                        last.then_inc(out_ready, 1)


def layer1_attention(nc, x, ident, keep, psum, wqk1, wv1, wo1, bo1, aux, key_aux, cosines, sines):
    with ExitStack() as ctx:
        sb = lambda n, s, d=FP32: ctx.enter_context(nc.sbuf_tensor(f"a1_{n}", s, d))
        xh, xl = sb("xh", [P, KC, TOK], FP32R), sb("xl", [P, KC, TOK], FP32R)
        layer_norm(nc, "n2", x, xh, xl, ident, psum)
        v_dram = nc.dram_tensor("v_scratch", [TT, P, G1 * HD1], FP32).ap()
        aux_dram = nc.dram_tensor("aux_scratch", [G1 * AUX, REP * SEQ], FP32).ap()

        with ExitStack() as prep:
            tb = lambda n, s, d=FP32: prep.enter_context(nc.sbuf_tensor(f"v1_{n}", s, d))
            sem = lambda n: prep.enter_context(nc.semaphore(f"v1_{n}"))
            raw = tb("raw", [P, KC, G1 * HD1])
            wh, wl = tb("wh", [P, KC, G1 * HD1], FP32R), tb("wl", [P, KC, G1 * HD1], FP32R)
            staged = tb("staged", [P, 4, G1 * HD1])
            aux_raw = tb("aux_raw", [G1 * AUX, REP * SEQ])
            aux_r = tb("aux_r", [G1 * AUX, REP * SEQ], FP32R)
            bias = tb("bias", [P, DM])
            w_loaded, a_loaded, b_loaded, split, v_seq, product, copied, a_done = map(
                sem, ("w_loaded", "a_loaded", "b_loaded", "split", "v_seq", "product", "copied", "a_done"))
            stored = [sem(f"stored{n}") for n in range(4)]
            a_stored = sem("a_stored")
            with nc.Block() as block:
                @block.sync
                def _(sp):
                    sp.dma_start(raw[:, :, :], wv1).then_inc(w_loaded, 16)
                    sp.dma_start(aux_raw[:, :], aux).then_inc(a_loaded, 16)
                    sp.dma_start(bias[:, :], bo1.partition_broadcast(P)).then_inc(b_loaded, 16)
                    for t in range(TT):
                        sp.wait_ge(copied, t + 1)
                        sp.dma_start(v_dram[t, :, :], staged[:, t % 4, :]).then_inc(stored[t % 4], 16)
                    sp.wait_ge(a_done, 1)
                    sp.dma_start(aux_dram, aux_r[:, :].bitcast(FP32)).then_inc(a_stored, 16)
                    sp.wait_ge(a_stored, 16)
                    for n in range(4):
                        sp.wait_ge(stored[n], 16 * (TT // 4))

                @block.vector
                def _(dve):
                    dve.wait_ge(w_loaded, 16)
                    nc.vector.tensor_copy(wh[:, :, :], raw[:, :, :]).then_inc(v_seq, 1)
                    dve.wait_ge(v_seq, 1)
                    nc.vector.tensor_tensor(wl[:, :, :], raw[:, :, :], wh[:, :, :], ALU.subtract).then_inc(split, 1)
                    dve.wait_ge(a_loaded, 16)
                    nc.vector.tensor_copy(aux_r[:, :], aux_raw[:, :]).then_inc(a_done, 1)
                    dve.wait_ge(b_loaded, 16)
                    for t in range(TT):
                        last = nc.vector.tensor_tensor(x[:, t, :], x[:, t, :], bias[:, :], ALU.add)
                    last.then_inc(v_seq, 1)

                @block.tensor
                def _(pe):
                    pe.wait_ge(split, 1)
                    for t in range(TT):
                        if t >= 4:
                            pe.wait_ge(copied, t - 3)
                        cols = slice(t * P, t * P + P)
                        three_pass(nc, psum[:, t % 4, :], [((xh[:, k, cols], xl[:, k, cols]), (wh[:, k, :], wl[:, k, :]))
                                                           for k in range(KC)]).then_inc(product, 1)

                @block.scalar
                def _(act):
                    for t in range(TT):
                        act.wait_ge(product, t + 1)
                        if t >= 4:
                            act.wait_ge(stored[t % 4], 16 * (t // 4))
                        nc.scalar.activation(staged[:, t % 4, :], psum[:, t % 4, :], ACT.Copy).then_inc(copied, 1)

        sem = lambda n: ctx.enter_context(nc.semaphore(f"a1_{n}"))
        queries = [sb(f"queries{p}", [P, 2, 2, SEQ], FP32R) for p in range(2)]
        keys_hh = [sb(f"keys_hh{b}", [P, SEQ], FP32R) for b in range(BATCH)]
        keys_la = [sb(f"keys_la{b}", [P, SEQ], FP32R) for b in range(BATCH)]
        values = [sb(f"values{b}", [P, NB, HD1]) for b in range(BATCH)]
        BUFFER = (None, 0, 1, 2, 0, 1, 3, 4)
        probs_buf = [sb(f"probs{n}", [P, 2, SEQ - P * BUFFER.index(n)]) for n in range(5)]
        totals = [sb(f"totals{p}", [P, 2, SEQ]) for p in range(2)]
        cos_sb, sin_sb = sb("cos", [P, SEQ]), sb("sin", [P, SEQ])
        straight, swapped = sb("straight", [P, 2, 512]), sb("swapped", [P, 2, 512])
        high, low = sb("high", [P, 2, 512], FP32R), sb("low", [P, 2, 512], FP32R)
        out_sb, den_sb = sb("out_sb", [P, SEQ]), sb("den_sb", [P, 512])
        recip = sb("recip", [P, NB, 2])
        context = sb("context", [P, NB, P])
        context_t = [sb(f"context_t{p}", [P, SEQ]) for p in range(2)]
        w_raw = sb("w_raw", [P, KC, (REP + 1) * HD1])
        wq_h, wq_l = sb("wq_h", [P, KC, REP * HD1], FP32R), sb("wq_l", [P, KC, REP * HD1], FP32R)
        wk_h, wk_l = sb("wk_h", [P, KC, 2, HD1], FP32R), sb("wk_l", [P, KC, 2, HD1], FP32R)
        wo_sb = sb("wo_sb", [P, 2, DM])
        ones = sb("ones", [P, 32])
        (w_loaded, w_split, wh_done, tables, wo_loaded, work_filled, work_free, scores_ready, tanhs_done, exps_done,
         masks_done, mixes_done, outs_free, turned, roped, split_done, high_done, setup, key_aux_in, summed) = map(sem, (
             "w_loaded", "w_split", "wh_done", "tables", "wo_loaded", "work_filled", "work_free", "scores_ready",
             "tanhs_done", "exps_done", "masks_done", "mixes_done", "outs_free", "turned", "roped", "split_done",
             "high_done", "setup", "key_aux_in", "summed"))
        zeros_set, adds_done = sem("zeros_set"), sem("adds_done")
        placed = [sem(f"placed{n}") for n in range(2)]
        aux_loaded = [sem(f"aux_loaded{p}") for p in range(2)]
        v_loaded = [sem(f"v_loaded{b}") for b in range(BATCH)]
        flat = psum[:, :, :].rearrange("p a b -> p (a b)")
        OUT = 4 * 512
        work_bank = lambda n: 6 + n % 2
        STEPS = 2 * NB
        NT = 2 * STEPS
        ADDS = 4 * (NB - 1)

        def added(n):
            return 3 + len([m for m in range(n + 1) if m % NB]) + min(0, n + 1)

        def probs(s, a):
            p, kb = divmod(s % STEPS, NB)
            return totals[p][:, a, :] if kb == 0 else probs_buf[BUFFER[kb]][:, a, 0:SEQ - P * kb]

        def plan(unit, n):
            halves = [[] for _ in range(2 * STEPS)]
            nxt = 1 - unit
            for it, h in zip([("q", unit, 1, 0), ("q", unit, 1, 1), ("q", nxt, 0, 0), ("q", nxt, 0, 1),
                              ("k", nxt, None, 0), ("k", nxt, None, 1)], (0, 2, 16, 18, 20, 22)):
                halves[h].append(it)
            end = [("sum",), ("den",), ("ctx", 0), ("ctx", 1), ("back", 0), ("back", 1)]
            for it, h1, h0 in zip(end, (3, 6, 8, 9, 11, 12), (19, 24, 26, 27, 29, 30)):
                halves[h1].append(it + (1, 1 - unit)[-2:])
                halves[h0].append(it + (0, unit)[-2:])
            for i, h in enumerate((14, 17, 21, 25)):
                halves[h].append(("wo", i, None, 1 - unit))
            numbered = []
            for half in halves:
                numbered.append([(n + i, it) for i, it in enumerate(half)])
                n += len(half)
            return numbered, n

        FIRST = [(0, ("q", 0, 0, 0)), (1, ("q", 0, 0, 1)), (2, ("k", 0, None, 0)), (3, ("k", 0, None, 1))]
        plan0, n1 = plan(0, len(FIRST))
        plan1, n2 = plan(1, n1)
        PLANS, PER = [plan0, plan1], n2 - len(FIRST)
        LAST = [(n2 + i, it) for i, it in enumerate(
            [("sum", 1, 1), ("den", 1, 1), ("ctx", 0, 1, 1), ("ctx", 1, 1, 1), ("back", 0, 1, 1), ("back", 1, 1, 1)] +
            [("wo", i, None, 1) for i in range(4)])]
        WO_ITEM = [n for half in plan0 for n, it in half if it[0] == "wo"][-1]
        ROPES, ROPES_FIRST = 6, len(FIRST)
        SPLIT_W = 3
        SCALAR_ITEMS = ("sum", "back")
        DELAY = 1

        def ropes(u):
            out, r = [], 0
            for step in range(STEPS):
                row = [(n, it) for n, it in PLANS[u][2 * step] if it[0] in "qk"]
                out.append([(r + i, n, it) for i, (n, it) in enumerate(row)])
                r += len(row)
            return out

        def needed(items, n, it):
            kind = {"den": ("sum",), "back": ("ctx", it[1]), "wo": ("back", 1)}.get(it[0])
            return kind and max(m for m, other in items if m < n and other[:len(kind)] == kind)

        def read_before(u, half, kind):
            mine = [n for halves in ([], plan0, plan1)[:u + 1] for items in halves for n, it in items if it[0] == kind]
            mine += [n for items in PLANS[u][:half] for n, it in items if it[0] == kind]
            return mine[-1] + 1 if mine else max(n for items in plan1 for n, it in items if it[0] == kind) + 1 - PER

        with nc.Block() as block:
            @block.sync
            def _(sp):
                def load_w(g):
                    sp.dma_start(w_raw[:, :, :], wqk1[bass.ds(g, 1), :, :].rearrange("o p (k n) -> p (o k) n", k=KC))\
                        .then_inc(w_loaded, 16)

                def load_aux(p, g):
                    sp.dma_start(queries[p][64:64 + AUX, 1, :, :].rearrange("p h n -> p (h n)").bitcast(FP32),
                                 aux_dram[bass.ds(g * AUX, AUX), p * 2 * SEQ:(p + 1) * 2 * SEQ])\
                        .then_inc(aux_loaded[p], 16)

                def load_v(b, g):
                    sp.dma_start(values[b][:, :, :],
                                 v_dram[b * NB:b * NB + NB, :, bass.ds(g * HD1, HD1)].rearrange("t p d -> p t d"))\
                        .then_inc(v_loaded[b], 16)

                def load_wo(g):
                    sp.dma_start(wo_sb[:, :, :], wo1[bass.ds(g, 1), :, :].rearrange("o p (k n) -> p (o k) n", k=2))\
                        .then_inc(wo_loaded, 16)

                def place(r, it):
                    _, _, p, h = it
                    sp.wait_ge(split_done, r)
                    cols = slice(h * 512, h * 512 + 512)
                    for a in range(2):
                        rows = slice(64 * a, 64 * a + 64)
                        sp.dma_start(queries[p][0:64, :, a, cols].bitcast(FP32),
                                     high[rows, h, :].bitcast(FP32).unsqueeze(1).broadcast_to([64, 2, 512]))\
                            .then_inc(placed[h], 16)
                        sp.dma_start(queries[p][64:128, 0, a, cols].bitcast(FP32),
                                     low[rows, h, :].bitcast(FP32)).then_inc(placed[h], 16)

                load_w(0)
                sp.dma_start(cos_sb[:, :], cosines).then_inc(tables, 16)
                sp.dma_start(sin_sb[:, :], sines).then_inc(tables, 16)
                sp.dma_start(out_sb[64:128, :], key_aux).then_inc(key_aux_in, 16)
                load_wo(0)
                load_v(0, 0)
                sp.wait_ge(zeros_set, 2)
                for p in range(2):
                    load_aux(p, 0)
                sp.wait_ge(w_split, 1)
                load_w(1)
                for r, (_, it) in enumerate(FIRST[0:2]):
                    place(r + 1, it)
                with sp.Fori(0, G1, 1) as g:
                    for u in range(2):
                        before = g * (2 * ROPES) + (ROPES * u + ROPES_FIRST)
                        sp.wait_ge(mixes_done, g * (2 * STEPS) + (STEPS * u + 3))
                        load_v(1 - u, (g + u) % G1)
                        place(before + 1, ("q", u, 1, 0))
                        place(before + 2, ("q", u, 1, 1))
                        if u == 1:
                            sp.wait_ge(w_split, g + 2)
                            load_w((g + 2) % G1)
                            sp.wait_ge(scores_ready, g * (2 * NT) + (NT + NT // 2))
                            load_aux(0, (g + 1) % G1)
                        place(before + 3, ("q", 1 - u, 0, 0))
                        place(before + 4, ("q", 1 - u, 0, 1))
                        if u == 0:
                            sp.wait_ge(work_filled, g * PER + (WO_ITEM + 1))
                            load_wo(g)
                    sp.wait_ge(scores_ready, g * (2 * NT) + 2 * NT)
                    load_aux(1, (g + 1) % G1)
                sp.wait_ge(w_loaded, 16 * (G1 + 2))
                for p in range(2):
                    sp.wait_ge(aux_loaded[p], 16 * (G1 + 1))
                sp.wait_ge(v_loaded[0], 16 * (G1 + 1))
                sp.wait_ge(v_loaded[1], 16 * G1)
                for n in range(2):
                    sp.wait_ge(placed[n], 64 * (4 * G1 + 1))

            @block.gpsimd
            def _(pool):
                pool.sem_inc(masks_done, 1)
                for p in range(2):
                    nc.gpsimd.memset(queries[p][64:128, 1, :, :].bitcast(FP32), 0.0).then_inc(zeros_set, 1)

                def rope(item_done, slot, it):
                    h = it[3]
                    pool.wait_ge(work_free, item_done + 1)
                    nc.gpsimd.tensor_tensor(swapped[:, slot, :], swapped[:, slot, :], sin_sb[:, h * 512:h * 512 + 512],
                                            ALU.mult).then_inc(roped, 1)

                pool.wait_ge(tables, 32)
                for r, (n, it) in enumerate(FIRST):
                    rope(n + 2, r % 2, it)
                with pool.Fori(0, G1, 1) as g:
                    for u in range(2):
                        for s, step in enumerate(ropes(u)):
                            for r, n, it in step:
                                rope(g * PER + (n + 2), r % 2, it)
                            pool.wait_ge(exps_done, g * (2 * NT) + (NT * u + 2 * s + 2))
                            part = probs(s, slice(0, 2))[:, :, 0:P]
                            nc.gpsimd.tensor_tensor(part, part, keep[:, :].unsqueeze(1).broadcast_to([P, 2, P]),
                                                    ALU.mult).then_inc(masks_done, 1)

            @block.scalar
            def _(act):
                act.sem_inc(tanhs_done, 2)

                def tanh(g, t):
                    s = t // 2
                    kb = s % NB
                    act.wait_ge(scores_ready, g * (2 * NT) + (t + 1))
                    if t % 2 == 0:
                        act.wait_ge(mixes_done, g * (2 * STEPS) + (s + 1))
                        act.wait_ge(adds_done, g * ADDS + added(s - 3))
                    nc.scalar.activation(probs(s, t % 2), flat[:, 1024 * (t % 2) + kb * P:1024 * (t % 2) + SEQ],
                                         ACT.Tanh, scale=1.0 / (30.0 * HD1 ** 0.5)).then_inc(tanhs_done, 1)

                def take_out(mixes, read):
                    act.wait_ge(mixes_done, mixes)
                    act.wait_ge(work_filled, read)
                    nc.scalar.activation(out_sb[:, :], flat[:, OUT:OUT + SEQ], ACT.Copy).then_inc(outs_free, 1)

                def copy_item(n, base, it):
                    act.wait_ge(work_filled, base + (n + 1))
                    act.wait_ge(work_free, base + (n + 2))
                    to = den_sb[:, :] if it[0] == "sum" else context_t[it[2]][:, 512 * it[1]:512 * it[1] + 512]
                    nc.scalar.activation(to, psum[:, work_bank(n), :], ACT.Copy).then_inc(work_free, 1)

                tanh(0, 0)
                with act.Fori(0, G1, 1) as g:
                    for t in range(2 * NT):
                        tanh(g, t + 1)
                        act.wait_ge(tanhs_done, g * (2 * NT) + (t + 3))
                        nc.scalar.activation(probs(t // 2, t % 2), probs(t // 2, t % 2), ACT.Exp, scale=30.0)\
                            .then_inc(exps_done, 1)
                        u, half = divmod(t, NT)
                        if half % (2 * NB) == 1:
                            take_out(g * (2 * STEPS) + (t // 2 + 3), g * PER + read_before(u, half, "ctx"))
                        for n, it in PLANS[u][half - 1] if half else []:
                            if it[0] in SCALAR_ITEMS:
                                copy_item(n, g * PER, it)
                take_out(2 * STEPS * G1 + 3, (G1 - 1) * PER + read_before(1, NT, "ctx"))
                for n, it in LAST:
                    if it[0] in SCALAR_ITEMS:
                        copy_item(n, (G1 - 1) * PER, it)

            @block.vector
            def _(dve):
                dve.wait_ge(key_aux_in, 16)
                for b in range(BATCH):
                    nc.vector.tensor_copy(keys_la[b][64:128, :], out_sb[64:128, :])
                nc.vector.memset(ones[:, :], 1.0).then_inc(setup, 1)
                nc.vector.memset(psum[:, 4:6, :], 0.0)
                nc.vector.memset(context_t[0][:, :], 0.0)
                nc.vector.memset(probs(NB - 1, slice(0, 2)), 0.0)
                nc.vector.memset(totals[1][:, :, :], 1.0)
                nc.vector.memset(values[1][:, :, :], 0.0).then_inc(setup, 1)
                dve.wait_ge(setup, 2)
                dve.sem_inc(adds_done, 2)

                def split_weights(nth):
                    dve.wait_ge(w_loaded, nth * 16)
                    nc.vector.tensor_copy(wq_h[:, :, :], w_raw[:, :, 0:REP * HD1])
                    nc.vector.tensor_copy(wk_h[:, :, :, :], w_raw[:, :, REP * HD1:].unsqueeze(2)
                                          .broadcast_to([P, KC, 2, HD1])).then_inc(wh_done, 1)
                    dve.wait_ge(wh_done, nth)
                    nc.vector.tensor_tensor(wq_l[:, :, :], w_raw[:, :, 0:REP * HD1], wq_h[:, :, :], ALU.subtract)
                    nc.vector.tensor_tensor(wk_l[:, :, :, :], w_raw[:, :, REP * HD1:].unsqueeze(2)
                                            .broadcast_to([P, KC, 2, HD1]), wk_h[:, :, :, :],
                                            ALU.subtract).then_inc(w_split, 1)

                def rotate(r, slot, it, n):
                    if r is not None:
                        dve.wait_ge(split_done, r - 2)
                    nc.vector.tensor_tensor(straight[:, slot, :], psum[:, work_bank(n), :],
                                            cos_sb[:, it[3] * 512:it[3] * 512 + 512], ALU.mult)
                    nc.vector.stream_shuffle(swapped[:, slot, :], psum[:, work_bank(n), :], [i ^ 1 for i in range(32)])\
                        .then_inc(work_free, 1)

                def split(r, slot, it, nth):
                    dve.wait_ge(roped, r)
                    nc.vector.tensor_tensor(straight[:, slot, :], straight[:, slot, :], swapped[:, slot, :],
                                            ALU.add).then_inc(summed, 1)
                    dve.wait_ge(summed, r)
                    h = it[3]
                    if it[0] == "q":
                        if nth is not None:
                            dve.wait_ge(placed[h], nth * 64)
                        nc.vector.tensor_copy(high[:, h, :], straight[:, slot, :]).then_inc(high_done, 1)
                        dve.wait_ge(high_done, r)
                        nc.vector.tensor_tensor(low[:, h, :], straight[:, slot, :], high[:, h, :],
                                                ALU.subtract).then_inc(split_done, 1)
                    else:
                        b, cols = it[1], slice(h * 512, h * 512 + 512)
                        nc.vector.tensor_copy(keys_hh[b][:, cols], straight[:, slot, :]).then_inc(high_done, 1)
                        dve.wait_ge(high_done, r)
                        nc.vector.tensor_tensor(keys_la[b][0:64, cols], straight[0:64, slot, :], keys_hh[b][0:64, cols],
                                                ALU.subtract).then_inc(split_done, 1)

                def add_up(g, n):
                    p, kb = divmod(n % STEPS, NB)
                    dve.wait_ge(masks_done, g * (2 * STEPS) + (n + 2))
                    dve.wait_ge(adds_done, g * ADDS + added(n - 1))
                    if kb == 1:
                        dve.wait_ge(mixes_done, g * (2 * STEPS) + (n + 3))
                    to = totals[p][:, :, kb * P:SEQ]
                    nc.vector.tensor_tensor(to, to, probs(n, slice(0, 2)), ALU.add).then_inc(adds_done, 1)

                def finish(n, it):
                    bank = psum[:, work_bank(n), :]
                    if it[0] == "den":
                        last = nc.vector.reciprocal(
                            recip[:, :, :].rearrange("p (j a) h -> p j a h", a=2),
                            bank.rearrange("p (j h a z) -> p j a h z", j=4, h=2, a=2)[:, :, :, :, 0])
                    elif it[0] == "ctx":
                        i = it[1]
                        last = nc.vector.tensor_tensor(
                            context[:, 4 * i:4 * i + 4, :].rearrange("p b (h d) -> p b h d", h=2),
                            bank.rearrange("p (b h d) -> p b h d", b=4, h=2),
                            recip[:, 4 * i:4 * i + 4, :].unsqueeze(3).broadcast_to([P, 4, 2, HD1]), ALU.mult)
                    else:
                        t = NB * it[3] + 2 * it[1]
                        last = nc.vector.tensor_tensor(x[:, t:t + 2, :], bank.rearrange("p (t d) -> p t d", t=2),
                                                       x[:, t:t + 2, :], ALU.add)
                    last.then_inc(work_free, 1)

                split_weights(1)
                dve.wait_ge(tables, 32)
                for r, (n, it) in enumerate(FIRST):
                    dve.wait_ge(work_filled, n + 1)
                    rotate(r + 1 if r >= 2 else None, r % 2, it, n)
                    if r > 0:
                        split(r, (r - 1) % 2, FIRST[r - 1][1], None)
                split(ROPES_FIRST, (ROPES_FIRST - 1) % 2, FIRST[-1][1], None)
                with dve.Fori(0, G1, 1) as g:
                    for u in range(2):
                        rows = ropes(u)
                        for s in range(STEPS):
                            for half in range(2):
                                for n, it in PLANS[u][2 * s + half]:
                                    if it[0] in SCALAR_ITEMS:
                                        continue
                                    dve.wait_ge(work_filled, g * PER + (n + 1))
                                    dve.wait_ge(work_free, g * PER + (n + 2))
                                    if it[0] in "qk":
                                        r = rows[s][0][0]
                                        rotate(g * (2 * ROPES) + (ROPES * u + ROPES_FIRST + r + 1), r % 2, it, n)
                                    else:
                                        finish(n, it)
                                if half == 0 and s % NB != 1:
                                    add_up(g, STEPS * u + s - 1)
                            if s >= DELAY:
                                for r, _, it in rows[s - DELAY]:
                                    split(g * (2 * ROPES) + (ROPES * u + ROPES_FIRST + r + 1), r % 2, it,
                                          g * 4 + (2 * u + r // 2 + 1))
                            if u == 1 and s == SPLIT_W:
                                split_weights(g + 2)
                add_up(G1 - 1, 2 * STEPS - 1)
                for n, it in LAST:
                    if it[0] in SCALAR_ITEMS:
                        continue
                    dve.wait_ge(work_filled, n + 1 + PER * (G1 - 1))
                    dve.wait_ge(work_free, n + 2 + PER * (G1 - 1))
                    finish(n, it)

            @block.tensor
            def _(pe):
                pe.sem_inc(work_free, 2)
                pe.sem_inc(mixes_done, 2)

                def item(n, base, it, need, weights, outs, turn, totals_at):
                    bank = psum[:, work_bank(n), :]
                    pe.wait_ge(work_free, base + (n + 1))
                    if need is not None:
                        pe.wait_ge(work_free, base + (need + 3))
                    if it[0] in "qk":
                        pe.wait_ge(w_split, weights)
                        _, b, p, h = it
                        cols = slice(b * SEQ + h * 512, b * SEQ + h * 512 + 512)
                        if it[0] == "q":
                            w = [(wq_h[:, k, p * P:p * P + P], wq_l[:, k, p * P:p * P + P]) for k in range(KC)]
                        else:
                            w = [(wk_h[:, k, :, :].rearrange("p c d -> p (c d)"),
                                  wk_l[:, k, :, :].rearrange("p c d -> p (c d)")) for k in range(KC)]
                        last = three_pass(nc, bank, [(w[k], (xh[:, k, cols], xl[:, k, cols])) for k in range(KC)])
                    elif it[0] == "sum":
                        pe.wait_ge(adds_done, totals_at)
                        for parity in range(2):
                            for a in range(2):
                                row = 32 * (2 * a + parity)
                                moving = totals[it[1]][:, a, :].rearrange("p (b q) -> p b q", q=P)
                                last = nc.tensor.matmul(psum[row:row + 32, work_bank(n), :], ones[:, :],
                                                        moving[:, parity::2, :], start=True, stop=True)
                    elif it[0] == "den":
                        for j in range(4):
                            last = nc.tensor.transpose(bank[:, j * P:j * P + P], den_sb[:, j * P:j * P + P], ident[:, :])
                    elif it[0] == "ctx":
                        pe.wait_ge(outs_free, outs)
                        for j in range(4):
                            at = (4 * it[1] + j) * P
                            last = nc.tensor.transpose(bank[:, j * P:j * P + P], out_sb[:, at:at + P], ident[:, :])
                    elif it[0] == "back":
                        for j in range(4):
                            last = nc.tensor.transpose(bank[:, j * P:j * P + P], context[:, 4 * it[1] + j, :], ident[:, :])
                    else:
                        if it[1] == 0:
                            pe.wait_ge(wo_loaded, turn * 16)
                        for j in range(2):
                            at = (2 * it[1] + j) * P
                            for p in range(2):
                                last = nc.tensor.matmul(bank[:, j * DM:j * DM + DM], context_t[p][:, at:at + P],
                                                        wo_sb[:, p, :], start=(p == 0), stop=(p == 1))
                    last.then_inc(work_filled, 1)

                def segments(kb):
                    return [(q0, q1) for q0, q1 in ((kb * P, 512), (max(kb * P, 512), SEQ)) if q0 < q1]

                def scores(g, u, t):
                    if t == NT // 2:
                        for h in range(2):
                            pe.wait_ge(placed[h], g * 256 + (128 * u + 128))
                        pe.wait_ge(aux_loaded[1], g * 16 + 16)
                    if t == NT:
                        for h in range(2):
                            pe.wait_ge(placed[h], g * 256 + (128 * u + 192))
                        pe.wait_ge(split_done, g * (2 * ROPES) + (ROPES * (u + 1) + ROPES_FIRST))
                        pe.wait_ge(aux_loaded[0], g * 16 + (16 * u + 16))
                    if t >= NT:
                        g, u, t = (g, 1, t - NT) if u == 0 else (g + 1, 0, t - NT)
                    s, a = divmod(t, 2)
                    p, kb = divmod(s, NB)
                    pe.wait_ge(tanhs_done, g * (2 * NT) + (NT * u + t + 1))
                    at = slice(kb * P, kb * P + P)
                    for q0, q1 in segments(kb):
                        to = flat[:, 1024 * a + q0:1024 * a + q1]
                        nc.tensor.matmul(to, keys_hh[u][:, at], queries[p][:, 0, a, q0:q1], start=True,
                                         stop=False)
                        last = nc.tensor.matmul(to, keys_la[u][:, at], queries[p][:, 1, a, q0:q1], start=False,
                                                stop=True)
                    last.then_inc(scores_ready, 1)

                def mix(g, u, s, part):
                    v = u if s >= 0 else 1 - u
                    p, kb = divmod(s, NB)
                    if part == len(segments(kb)):
                        return
                    q0, q1 = segments(kb)[part]
                    pe.wait_ge(masks_done, g * (2 * STEPS) + (STEPS * u + s + 2))
                    if kb == 0:
                        pe.wait_ge(outs_free, g * 4 + (2 * u + p + 1))
                    if s == 0:
                        pe.wait_ge(v_loaded[u], g * 16 + 16)
                    for a in range(2):
                        last = nc.tensor.matmul(flat[64 * a:64 * a + 64, OUT + q0:OUT + q1], values[v][:, kb, :],
                                                probs(s, a)[:, q0 - kb * P:q1 - kb * P], start=(kb == 0),
                                                stop=(kb == (3 if q1 == 512 else NB - 1)))
                    if q1 == SEQ:
                        last.then_inc(mixes_done, 1)

                pe.wait_ge(setup, 2)
                pe.wait_ge(zeros_set, 2)
                for n, it in FIRST:
                    item(n, 0, it, None, 1, 0, 0, 0)
                for h in range(2):
                    pe.wait_ge(placed[h], 64)
                pe.wait_ge(split_done, ROPES_FIRST)
                pe.wait_ge(aux_loaded[0], 16)
                scores(0, 0, 0)
                scores(0, 0, 1)
                for a in range(2):
                    nc.tensor.matmul(flat[64 * a:64 * a + 64, OUT + 512:OUT + SEQ], values[1][:, 0, :],
                                     context_t[0][:, 0:512], start=True, stop=False)
                with pe.Fori(0, G1, 1) as g:
                    for u in range(2):
                        for s in range(STEPS):
                            for half in range(2):
                                scores(g, u, 2 * s + 2 + half)
                                for n, it in PLANS[u][2 * s + half]:
                                    item(n, g * PER, it, needed(sum(PLANS[u], []), n, it),
                                         g + (1 + (u == 1 and s >= NB)), g * 4 + (2 * u + s // NB + 1), g + (u + 1),
                                         g * ADDS + added(STEPS * u + s // NB * NB - 1))
                                mix(g, u, s - 1, half)
                mix(G1 - 1, 1, STEPS - 1, 0)
                for n, it in LAST:
                    item(n, PER * (G1 - 1), it, needed(LAST, n, it), 0, 4 * G1 + 1, G1 + 1,
                         G1 * ADDS + added(-1))


def expert_ffn(nc, x, ident, psum, w1, b1, w2, b2, vt, u, select):
    with ExitStack() as ctx:
        sb = lambda n, s, d=FP32: ctx.enter_context(nc.sbuf_tensor(f"f1_{n}", s, d))
        sem = lambda n: ctx.enter_context(nc.semaphore(f"f1_{n}"))
        xh, xl = sb("xh", [P, KC, TOK], FP32R), sb("xl", [P, KC, TOK], FP32R)
        layer_norm(nc, "n3", x, xh, xl, ident, psum)
        w1_raw, v_raw = sb("w1_raw", [P, KC, DM]), sb("v_raw", [P, KC, ER * P])
        w1_h, w1_l = sb("w1_h", [P, KC, DM], FP32R), sb("w1_l", [P, KC, DM], FP32R)
        v_h, v_l = sb("v_h", [P, KC, ER * P], FP32R), sb("v_l", [P, KC, ER * P], FP32R)
        select_raw, select_sb = sb("select_raw", [P, ER, P]), sb("select", [P, ER, P], FP32R)
        w2_sb, u_sb = sb("w2", [P, KC, EXPERTS]), sb("u", [P, ER, DM])
        b1_sb, b2_sb = sb("b1", [P, KC]), sb("b2", [P, EXPERTS])
        hidden = sb("hidden", [P, KC, 512])
        vx = sb("vx", [P, ER, 512])
        logits, alphas = sb("logits", [P, 4, EXPERTS]), sb("alphas", [P, 4, EXPERTS])
        top, total = sb("top", [P, 4]), sb("total", [P, 4])
        alpha_h, alpha_l = sb("alpha_h", [P, 512], FP32R), sb("alpha_l", [P, 512], FP32R)
        mixed = sb("mixed", [P, ER, 512])
        loaded = [sem(f"loaded{n}") for n in range(4)]
        (v_seq, weights_ready, hidden_ready, hidden_done, vx_ready, vx_copied, logits_ready, shifted, exps_done,
         alphas_ready, turned, alpha_split, spread, mixed_done, out_ready, added) = map(sem, (
             "v_seq", "weights_ready", "hidden_ready", "hidden_done", "vx_ready", "vx_copied", "logits_ready",
             "shifted", "exps_done", "alphas_ready", "turned", "alpha_split", "spread", "mixed_done", "out_ready",
             "added"))
        BLOCKS = TOK // 512
        SETUP = 8
        PER = 5
        with nc.Block() as block:
            @block.sync
            def _(sp):
                for n, (to, of) in enumerate(((w1_raw, w1), (v_raw, vt), (select_raw, select))):
                    sp.dma_start(to[:, :, :], of).then_inc(loaded[n], 16)
                sp.dma_start(w2_sb[:, :, :], w2).then_inc(loaded[3], 16)
                sp.dma_start(u_sb[:, :, :], u).then_inc(loaded[3], 16)
                sp.dma_start(b1_sb[:, :], b1).then_inc(loaded[3], 16)
                sp.dma_start(b2_sb[:, :], b2.partition_broadcast(P)).then_inc(loaded[3], 16)

            @block.vector
            def _(dve):
                v = Chain(dve, v_seq)
                for n, (raw, h, l) in enumerate(((w1_raw, w1_h, w1_l), (v_raw, v_h, v_l))):
                    dve.wait_ge(loaded[n], 16)
                    v.link(nc.vector.tensor_copy(h[:, :, :], raw[:, :, :]))
                    v.link(nc.vector.tensor_tensor(l[:, :, :], raw[:, :, :], h[:, :, :], ALU.subtract))
                dve.wait_ge(loaded[2], 16)
                v.link(nc.vector.tensor_copy(select_sb[:, :, :], select_raw[:, :, :]))
                v.link(nc.vector.memset(alpha_h[:, :].bitcast(FP32), 0.0))
                v.link(nc.vector.memset(alpha_l[:, :].bitcast(FP32), 0.0))
                dve.wait_ge(loaded[3], 64)
                v.link(nc.vector.memset(total[:, :], 0.0))
                assert v.n == SETUP
                with dve.Fori(0, BLOCKS, 1) as i:
                    v = Chain(dve, v_seq, i * PER + SETUP)
                    for c in range(ER):
                        dve.wait_ge(vx_ready, i * ER + (c + 1))
                        nc.vector.tensor_copy(vx[:, c, :], psum[:, 2 + c, :]).then_inc(vx_copied, 1)
                    dve.wait_ge(logits_ready, i + 1)
                    v.link(nc.vector.tensor_tensor(logits[:, :, :],
                                                   psum[:, 6, 0:4 * EXPERTS].rearrange("p (t e) -> p t e", t=4),
                                                   b2_sb[:, :].unsqueeze(1).broadcast_to([P, 4, EXPERTS]), ALU.add))
                    v.link(nc.vector.reduce_max(top[:, :], logits[:, :, :], AXIS.X))
                    nc.vector.tensor_tensor(logits[:, :, :], logits[:, :, :],
                                            top[:, :].unsqueeze(2).broadcast_to([P, 4, EXPERTS]),
                                            ALU.subtract).then_inc(shifted, 1)
                    dve.wait_ge(exps_done, i + 1)
                    v.link(nc.vector.reduce_sum(total[:, :], alphas[:, :, :], AXIS.X))
                    v.link(nc.vector.reciprocal(total[:, :], total[:, :]))
                    nc.vector.tensor_tensor(alphas[:, :, :], alphas[:, :, :],
                                            total[:, :].unsqueeze(2).broadcast_to([P, 4, EXPERTS]),
                                            ALU.mult).then_inc(alphas_ready, 1)
                    dve.wait_ge(turned, i + 1)
                    v.link(nc.vector.tensor_copy(alpha_h[0:EXPERTS, :], psum[0:EXPERTS, 7, :]))
                    nc.vector.tensor_tensor(alpha_l[0:EXPERTS, :], psum[0:EXPERTS, 7, :], alpha_h[0:EXPERTS, :],
                                            ALU.subtract).then_inc(alpha_split, 1)
                    for c in range(ER):
                        dve.wait_ge(spread, i * ER + (c + 1))
                        nc.vector.tensor_tensor(mixed[:, c, :], psum[:, 6 * (c % 2), :], vx[:, c, :], ALU.mult)\
                            .then_inc(mixed_done, 1)
                    for t in range(4):
                        dve.wait_ge(out_ready, i * 4 + (t + 1))
                        rows = x[:, bass.ds(i * 4 + t, 1), :]
                        nc.vector.tensor_tensor(rows, psum[:, 2 + t:3 + t, 0:DM], rows, ALU.add).then_inc(added, 1)

            @block.scalar
            def _(act):
                act.wait_ge(v_seq, SETUP)
                with act.Fori(0, BLOCKS, 1) as i:
                    for m in range(KC):
                        act.wait_ge(hidden_ready, i * KC + (m + 1))
                        nc.scalar.activation(hidden[:, m, :], psum[:, m, :], ACT.Relu, bias=b1_sb[:, m:m + 1])\
                            .then_inc(hidden_done, 1)
                    act.wait_ge(shifted, i + 1)
                    nc.scalar.activation(alphas[:, :, :], logits[:, :, :], ACT.Exp).then_inc(exps_done, 1)

            @block.tensor
            def _(pe):
                pe.sem_inc(added, 4)
                pe.sem_inc(mixed_done, 2)
                pe.wait_ge(v_seq, SETUP)
                with pe.Fori(0, BLOCKS, 1) as i:
                    cols = bass.ds(i * 512, 512)
                    pe.wait_ge(mixed_done, i * ER + 2)
                    for m in range(KC):
                        at = slice(m * P, m * P + P)
                        three_pass(nc, psum[:, m, :], [((w1_h[:, k, at], w1_l[:, k, at]), (xh[:, k, cols], xl[:, k, cols]))
                                                       for k in range(KC)]).then_inc(hidden_ready, 1)
                    for c in range(ER):
                        at = slice(c * P, c * P + P)
                        pe.wait_ge(added, i * 4 + (c + 1))
                        three_pass(nc, psum[:, 2 + c, :], [((v_h[:, k, at], v_l[:, k, at]),
                                                            (xh[:, k, cols], xl[:, k, cols]))
                                                           for k in range(KC)]).then_inc(vx_ready, 1)
                    pe.wait_ge(hidden_done, i * KC + KC)
                    for t in range(4):
                        for k in range(KC):
                            last = nc.tensor.matmul(psum[:, 6, EXPERTS * t:EXPERTS * t + EXPERTS],
                                                    hidden[:, k, t * P:t * P + P], w2_sb[:, k, :],
                                                    start=(k == 0), stop=(k == KC - 1))
                    last.then_inc(logits_ready, 1)
                    pe.wait_ge(alphas_ready, i + 1)
                    for t in range(4):
                        last = nc.tensor.transpose(psum[0:EXPERTS, 7, t * P:t * P + P], alphas[:, t, :], ident[:, :])
                    last.then_inc(turned, 1)
                    pe.wait_ge(alpha_split, i + 1)
                    for c in range(ER):
                        pe.wait_ge(mixed_done, i * ER + (c + 1))
                        nc.tensor.matmul(psum[:, 6 * (c % 2), :], select_sb[:, c, :], alpha_h[:, :], start=True,
                                         stop=False)
                        nc.tensor.matmul(psum[:, 6 * (c % 2), :], select_sb[:, c, :], alpha_l[:, :], start=False,
                                         stop=True).then_inc(spread, 1)
                    pe.wait_ge(mixed_done, i * ER + (ER + 2))
                    for t in range(4):
                        pe.wait_ge(vx_copied, i * ER + ER)
                        for c in range(ER):
                            last = nc.tensor.matmul(psum[:, 2 + t, 0:DM], mixed[:, c, t * P:t * P + P], u_sb[:, c, :],
                                                    start=(c == 0), stop=(c == ER - 1))
                        last.then_inc(out_ready, 1)


def constants():
    import numpy as np

    def parts(v):
        out, rest = [], np.asarray(v, np.float64)
        for _ in range(3):
            bits = rest.astype(np.float32).view(np.uint32) & np.uint32(0xFFFFF000)
            out.append(bits.view(np.float32))
            rest = rest - out[-1].astype(np.float64)
        return out

    half = HD1 // 2
    inverse = (np.float32(1.0) / np.float32(10000.0) ** (np.arange(0, HD1, 2, dtype=np.float32) / np.float32(HD1)))
    angles = (np.arange(SEQ, dtype=np.float32)[:, None] * inverse.astype(np.float32)[None, :]).astype(np.float32)
    cosines = np.repeat(np.cos(angles.astype(np.float64)).astype(np.float32), 2, axis=1).T
    sines = np.repeat(np.sin(angles.astype(np.float64)).astype(np.float32), 2, axis=1).T
    sines = sines * np.where(np.arange(HD1) % 2 == 0, -1, 1).astype(np.float32)[:, None]
    slopes = (2.0 ** (-(np.arange(1, H1 + 1) * 8.0 / H1))).astype(np.float32).astype(np.float64)
    position = np.arange(SEQ, dtype=np.float64)
    aux = np.zeros((G1, AUX, REP, SEQ), np.float32)
    for h in range(H1):
        for n, part in enumerate(parts(slopes[h] * position) + parts(slopes[h] * np.ones(SEQ))):
            aux[h // REP, n, h % REP] = part
    key_aux = np.zeros((HD1, SEQ), np.float32)
    key_aux[0:3] = -1.0
    key_aux[3:6] = position
    select = np.zeros((P, ER, P), np.float32)
    for c in range(ER):
        for m in range(P):
            select[(c * P + m) // RANK, c, m] = 1.0
    return {"cosines": np.concatenate([cosines, cosines]), "sines": np.concatenate([sines, sines]),
            "aux": aux.reshape(G1 * AUX, REP * SEQ), "key_aux": key_aux, "select": select}


def build(nc, a, out):
    with ExitStack() as ctx:
        sb = lambda n, s, d=FP32: ctx.enter_context(nc.sbuf_tensor(n, s, d))
        sem = lambda n: ctx.enter_context(nc.semaphore(n))
        psum = ctx.enter_context(nc.psum_tensor("psum", [P, 8, 512], FP32))
        x = sb("rows", [P, TT, DM])
        ident = sb("ident", [P, P])
        ident_b = sb("ident_b", [P, P], BF16)
        mask_q = sb("mask_q", [P, P], BF16)
        mask_k = sb("mask_k", [P, P], BF16)
        keep = sb("keep", [P, P])
        loaded, made, stored = map(sem, ("loaded", "made", "stored"))
        with nc.Block() as block:
            @block.sync
            def _(sp):
                sp.dma_start(x[:, :, :], a["x"]).then_inc(loaded, 16)
                sp.wait_ge(loaded, 16)

            @block.gpsimd
            def _(pool):
                for n, t in enumerate((ident, ident_b, mask_q, mask_k, keep)):
                    nc.gpsimd.memset(t[:, :], 1.0 if n == 4 else 0.0).then_inc(made, 1)
                    pool.wait_ge(made, 2 * n + 1)
                    if n < 2:
                        nc.gpsimd.affine_select(out=t[:, :], in_=t[:, :], compare_op=ALU.not_equal, fill=1.0, base=0,
                                                pattern=[[-1, P]], channel_multiplier=1).then_inc(made, 1)
                    else:
                        sign = 1 if n == 2 else -1
                        nc.gpsimd.affine_select(out=t[:, :], in_=t[:, :], compare_op=ALU.is_ge, base=0,
                                                fill=-1e30 if n < 4 else 0.0,
                                                pattern=[[-sign, P]], channel_multiplier=sign).then_inc(made, 1)
                    pool.wait_ge(made, 2 * n + 2)

        layer0_attention(nc, x, ident, ident_b, mask_q, mask_k, psum, a["wq0"], a["wk0"], a["wv0"], a["wo0"])
        ternary_ffn(nc, x, ident, psum, a["w1"], a["w3"], a["w2"])
        layer1_attention(nc, x, ident, keep, psum, a["wqk1"], a["wv1"], a["wo1"], a["bo1"], a["aux"], a["key_aux"],
                         a["cosines"], a["sines"])
        expert_ffn(nc, x, ident, psum, a["e_w1"], a["e_b1"], a["e_w2"], a["e_b2"], a["e_vt"], a["e_u"], a["select"])
        with nc.Block() as block:
            @block.sync
            def _(sp):
                sp.dma_start(out, x[:, :, :]).then_inc(stored, 16)
                sp.wait_ge(stored, 16)


def kernel(**inputs):
    import numpy as np
    import concourse.bacc as bacc
    from concourse.bass_utils import run_bass_kernel_spmd

    def rows(w):
        w = np.ascontiguousarray(w)
        return np.ascontiguousarray(w.reshape(-1, P, w.shape[1]).transpose(1, 0, 2))

    i = {k: np.asarray(v) for k, v in inputs.items()}
    arrays = {
        "x": np.ascontiguousarray(i["L0_attn_x"].reshape(TT, P, DM).transpose(1, 0, 2)),
        "wq0": rows(i["L0_attn_wq"].T), "wk0": rows(i["L0_attn_wk"].T), "wv0": rows(i["L0_attn_wv"].T),
        "wo0": rows(i["L0_attn_wo"].T),
        "w1": rows(np.pad(i["L0_ffn_w1"], ((0, HC * P - HID), (0, 0))).T),
        "w3": rows(np.pad(i["L0_ffn_w3"], ((0, HC * P - HID), (0, 0))).T),
        "w2": rows(np.pad(i["L0_ffn_w2"], ((0, 0), (0, HC * P - HID))).T),
        "wqk1": np.ascontiguousarray(np.concatenate(
            [i["L1_attn_Wq"].reshape(KC, P, G1, REP * HD1), i["L1_attn_Wk"].reshape(KC, P, G1, HD1)], axis=3)
            .transpose(2, 1, 0, 3)).reshape(G1, P, KC * (REP + 1) * HD1),
        "wv1": rows(i["L1_attn_Wv"]),
        "wo1": np.ascontiguousarray(i["L1_attn_Wo"].reshape(G1, 2, P, DM).transpose(0, 2, 1, 3)).reshape(G1, P, 2 * DM),
        "bo1": i["L1_attn_bo"],
        "e_w1": rows(i["L1_ffn_W1"]), "e_w2": rows(i["L1_ffn_W2"]),
        "e_b1": np.ascontiguousarray(i["L1_ffn_b1"].reshape(KC, P).T), "e_b2": i["L1_ffn_b2"],
        "e_vt": rows(i["L1_ffn_V"].reshape(EXPERTS * RANK, DM).T),
        "e_u": rows(i["L1_ffn_U"].transpose(0, 2, 1).reshape(EXPERTS * RANK, DM)),
        **constants(),
    }
    nc = bacc.Bacc("TRN2", target_bir_lowering=False, num_devices=1)
    a = {n: nc.dram_tensor(n, list(v.shape), FP32, kind="ExternalInput").ap() for n, v in arrays.items()}
    out = nc.dram_tensor("out", [P, TT, DM], FP32, kind="ExternalOutput").ap()
    build(nc, a, out)
    got = run_bass_kernel_spmd(nc, [arrays], core_ids=[0]).results[0]["out"]
    return np.asarray(got).transpose(1, 0, 2).reshape(BATCH, SEQ, DM)
```
